# Optimizing a Trainium2 kernel written in Bass

```python
import numpy as np
import jax
import jax.numpy as jnp

def _softmax(x, axis=-1):
    return jax.nn.softmax(x, axis=axis)

def _gelu(x):
    return jax.nn.gelu(x, approximate=True)

def _silu(x):
    return jax.nn.silu(x)

def _sigmoid(x):
    return jax.nn.sigmoid(x)

def _layernorm(x, axis=-1, eps=1e-05):
    m = jnp.mean(x, axis=axis, keepdims=True)
    v = jnp.var(x, axis=axis, keepdims=True)
    return (x - m) / jnp.sqrt(v + eps)

def _scatter_add(tgt, idx, src, axis=0):
    return tgt.at[idx].add(src)

def _segment_sum(src, seg, n):
    return jax.ops.segment_sum(src, seg, n)
kernel_name = 'mk_adj_preln_d4_adj_r2_9affea'

def setup_inputs(seed: int=0):
    np.random.seed(seed)
    _w = jnp.asarray

    def _rec_inputs():
        import jax
        import jax.numpy as jnp
        _gk = jax.random.key(seed)
        x = 0.0001732 + 1 * jax.random.normal(jax.random.fold_in(_gk, 1), (5120, 64), jnp.float32)
        _a = jax.random.bernoulli(jax.random.fold_in(_gk, 2), 0.00078125, (5120, 5120))
        _a = jnp.logical_or(_a, jnp.swapaxes(_a, -1, -2))
        _a = jnp.logical_or(_a, jnp.eye(5120, dtype=bool))
        _af = _a.astype(jnp.float32)
        _af = _af * jax.random.uniform(jax.random.fold_in(_gk, 3), (5120, 5120), jnp.float32, 0.05, 0.02)
        adj = _af
        return (x, adj)
    x, adj = _rec_inputs()

    def _L0_gnn_setup():
        import jax, jax.numpy as jnp
        import numpy as np
        N_USERS = 2048
        N_ITEMS = 3072
        EMB = 64
        LN_EPS = 1e-05
        key = jax.random.key(seed)
        ks = jax.random.split(key, 10)
        N = N_USERS + N_ITEMS
        ego = jax.random.normal(ks[0], (N, EMB), jnp.float32)
        adj = (jax.random.uniform(ks[1], (N, N), jnp.float32) < 0.01).astype(jnp.float32) * 0.02
        xav = float(np.sqrt(6.0 / (EMB + EMB)))
        W_u = jax.random.uniform(ks[2], (EMB, EMB), jnp.float32, -xav, xav)
        W_i = jax.random.uniform(ks[3], (EMB, EMB), jnp.float32, -xav, xav)
        diag_u = jax.random.uniform(ks[4], (N_USERS,), jnp.float32, 0.99, 1.01)
        diag_i = jax.random.uniform(ks[5], (N_ITEMS,), jnp.float32, 0.99, 1.01)
        par_u = jax.random.uniform(ks[6], (2,), jnp.float32, 0.0, 0.99)
        par_i = jax.random.uniform(ks[7], (2,), jnp.float32, 0.0, 0.99)
        ln_gamma = jnp.ones((EMB,), jnp.float32)
        ln_beta = jnp.zeros((EMB,), jnp.float32)
        return {'ego_embeddings': ego, 'adj': adj, 'W_u': W_u, 'diag_u': diag_u, 'par_u': par_u, 'W_i': W_i, 'diag_i': diag_i, 'par_i': par_i, 'ln_gamma': ln_gamma, 'ln_beta': ln_beta}
    _L0_gnn_all = _L0_gnn_setup()
    _L0_gnn_in = {k: v for k, v in _L0_gnn_all.items() if k in ('W_u', 'diag_u', 'par_u', 'W_i', 'diag_i', 'par_i', 'ln_gamma', 'ln_beta')}
    del _L0_gnn_all

    def _L1_gnn_setup():
        import jax, jax.numpy as jnp
        import numpy as np
        N = 5000
        DIM = 64
        F_CONST = 1.0
        B_CONST = 0.1
        R_CONST = 0.01
        key = jax.random.key(seed)
        k1, k2 = jax.random.split(key)
        t = jnp.zeros((1,), dtype=jnp.float32)
        x = jax.random.uniform(k1, (N, DIM), dtype=jnp.float32)
        A = jax.random.uniform(k2, (N, N), dtype=jnp.float32)
        return {'t': t, 'x': x, 'A': A}
    _L1_gnn_all = _L1_gnn_setup()
    _L1_gnn_in = {k: v for k, v in _L1_gnn_all.items() if k in ('t',)}
    del _L1_gnn_all

    def _L2_gnn_setup():
        import jax, jax.numpy as jnp
        import numpy as np
        N, IN_F, OUT_F, K = (8192, 64, 64, 4)
        key = jax.random.key(seed)
        k1, k2, k3 = jax.random.split(key, 3)
        x = jax.random.normal(k1, (N, IN_F), dtype=jnp.float32)
        L_scaled = jax.random.normal(k2, (N, N), dtype=jnp.float32) / np.sqrt(N)
        fan_in, fan_out = (K * IN_F, OUT_F)
        bound = np.sqrt(6.0 / (fan_in + fan_out))
        weight = jax.random.uniform(k3, (K, IN_F, OUT_F), dtype=jnp.float32, minval=-bound, maxval=bound)
        bias = jnp.zeros((OUT_F,), dtype=jnp.float32)
        return {'x': x, 'L_scaled': L_scaled, 'weight': weight, 'bias': bias}
    _L2_gnn_all = _L2_gnn_setup()
    _L2_gnn_in = {k: v for k, v in _L2_gnn_all.items() if k in ('weight', 'bias')}
    del _L2_gnn_all

    def _L3_gnn_setup():
        import jax, jax.numpy as jnp
        import numpy as np
        N, D_IN, D_OUT = (8192, 64, 64)
        AVG_DEG = 32.0
        L2_EPS = 1e-12
        key = jax.random.key(seed)
        kx, ka, kw, kb = jax.random.split(key, 4)
        X = jax.random.normal(kx, (N, D_IN), dtype=jnp.float32)
        adj = (jax.random.uniform(ka, (N, N)) < AVG_DEG / N).astype(jnp.float32)
        bound = 1.0 / np.sqrt(2 * D_IN)
        W = jax.random.uniform(kw, (2 * D_IN, D_OUT), dtype=jnp.float32, minval=-bound, maxval=bound)
        b = jax.random.uniform(kb, (D_OUT,), dtype=jnp.float32, minval=-bound, maxval=bound)
        return {'X': X, 'adj': adj, 'W': W, 'b': b}
    _L3_gnn_all = _L3_gnn_setup()
    _L3_gnn_in = {k: v for k, v in _L3_gnn_all.items() if k in ('W', 'b')}
    del _L3_gnn_all
    return {'x': x, 'adj': adj, 'L0_gnn_W_u': _L0_gnn_in['W_u'], 'L0_gnn_diag_u': _L0_gnn_in['diag_u'], 'L0_gnn_par_u': _L0_gnn_in['par_u'], 'L0_gnn_W_i': _L0_gnn_in['W_i'], 'L0_gnn_diag_i': _L0_gnn_in['diag_i'], 'L0_gnn_par_i': _L0_gnn_in['par_i'], 'L0_gnn_ln_gamma': _L0_gnn_in['ln_gamma'], 'L0_gnn_ln_beta': _L0_gnn_in['ln_beta'], 'L1_gnn_t': _L1_gnn_in['t'], 'L2_gnn_weight': _L2_gnn_in['weight'], 'L2_gnn_bias': _L2_gnn_in['bias'], 'L3_gnn_W': _L3_gnn_in['W'], 'L3_gnn_b': _L3_gnn_in['b']}

def reference(x, adj, L0_gnn_W_u, L0_gnn_diag_u, L0_gnn_par_u, L0_gnn_W_i, L0_gnn_diag_i, L0_gnn_par_i, L0_gnn_ln_gamma, L0_gnn_ln_beta, L1_gnn_t, L2_gnn_weight, L2_gnn_bias, L3_gnn_W, L3_gnn_b):
    import jax
    import jax.numpy as jnp

    def _L0_gnn_ref(ego_embeddings, adj, W_u, diag_u, par_u, W_i, diag_i, par_i, ln_gamma, ln_beta):
        import jax, jax.numpy as jnp
        import numpy as np
        N_USERS = 2048
        N_ITEMS = 3072
        EMB = 64
        LN_EPS = 1e-05
        nu = diag_u.shape[0]
        res = ego_embeddings
        ego_u = ego_embeddings[:nu]
        ego_i = ego_embeddings[nu:]
        u = par_u[0] * par_u[1] * (diag_u[:, None] * ego_u @ W_u) + ego_u
        i = par_i[0] * par_i[1] * (diag_i[:, None] * ego_i @ W_i) + ego_i
        e = jnp.concatenate([u, i], axis=0)
        h = adj @ (adj.T @ e)
        mu = jnp.mean(h, axis=-1, keepdims=True)
        var = jnp.var(h, axis=-1, keepdims=True)
        out = (h - mu) * jax.lax.rsqrt(var + LN_EPS) * ln_gamma + ln_beta + res
        return out

    def _L1_gnn_ref(t, x, A):
        import jax, jax.numpy as jnp
        import numpy as np
        N = 5000
        DIM = 64
        F_CONST = 1.0
        B_CONST = 0.1
        R_CONST = 0.01
        Ax = A @ x
        outer = R_CONST * jnp.sum(x * Ax, axis=1, keepdims=True)
        return F_CONST - B_CONST * x - outer

    def _L2_gnn_ref(x, L_scaled, weight, bias):
        import jax, jax.numpy as jnp
        import numpy as np
        N, IN_F, OUT_F, K = (8192, 64, 64, 4)
        Tx_prev2 = x
        Tx_prev1 = L_scaled @ x
        out = Tx_prev2 @ weight[0]
        if K > 1:
            out = out + Tx_prev1 @ weight[1]
        for k in range(2, K):
            Tx_curr = 2.0 * (L_scaled @ Tx_prev1) - Tx_prev2
            out = out + Tx_curr @ weight[k]
            Tx_prev2, Tx_prev1 = (Tx_prev1, Tx_curr)
        return out + bias

    def _L3_gnn_ref(X, adj, W, b):
        import jax, jax.numpy as jnp
        import numpy as np
        N, D_IN, D_OUT = (8192, 64, 64)
        AVG_DEG = 32.0
        L2_EPS = 1e-12
        deg = jnp.clip(jnp.sum(adj, axis=1, keepdims=True) + 1.0, 1.0, None)
        h_neigh = (adj @ X + X) / deg
        concat = jnp.concatenate([X, h_neigh], axis=1)
        z = concat @ W + b
        out = jax.nn.relu(z)
        norm = jnp.linalg.norm(out, axis=1, keepdims=True)
        return out / jnp.maximum(norm, L2_EPS)
    h = jnp.maximum(_layernorm(x, axis=-1), 0.0)
    x = x + _L0_gnn_ref(h, adj, L0_gnn_W_u, L0_gnn_diag_u, L0_gnn_par_u, L0_gnn_W_i, L0_gnn_diag_i, L0_gnn_par_i, L0_gnn_ln_gamma, L0_gnn_ln_beta)
    h = jnp.maximum(_layernorm(x, axis=-1), 0.0)
    x = x + _L1_gnn_ref(L1_gnn_t, h, adj)
    h = jnp.maximum(_layernorm(x, axis=-1), 0.0)
    x = x + _L2_gnn_ref(h, adj, L2_gnn_weight, L2_gnn_bias)
    h = jnp.maximum(_layernorm(x, axis=-1), 0.0)
    x = x + _L3_gnn_ref(h, adj, L3_gnn_W, L3_gnn_b)
    return x

_drawn_inputs = setup_inputs


def setup_inputs(seed=0):
    import zlib

    import numpy as np

    out = dict(_drawn_inputs(seed))
    spreads = {'L0_gnn_ln_gamma': (1.0, 0.2), 'L0_gnn_ln_beta': (0.0, 0.1), 'L2_gnn_bias': (0.0, 0.1)}
    factors = {'L0_gnn_diag_u': 8.0, 'L0_gnn_diag_i': 8.0, 'L3_gnn_b': 8.0}
    for name, (base, spread) in spreads.items():
        noise = np.random.default_rng([zlib.crc32(name.encode()), seed]).standard_normal(out[name].shape)
        drawn = base * np.exp(spread * noise) if base else spread * noise
        out[name] = jnp.asarray(drawn.astype(out[name].dtype))
    for name, factor in factors.items():
        out[name] = (out[name] * factor).astype(out[name].dtype)
    return out
```

```python
from contextlib import ExitStack

import concourse.bass as bass
from concourse import mybir

P = 128
D = 64
BW = 512
Q = BW // P
N = 5120
NB = N // BW
NT = N // P
CH = 2 * Q
NC = NT // CH
NU = 2048
EPS = 1e-5
A_SLOTS = 5
DIAG = [A_SLOTS + NB - 1, A_SLOTS + NB]
SLOTS = A_SLOTS + NB + 1
RING = [NB, NB + 1, NB + 2, NB + 3, 8, 9, 6, 7, 4, 5, 2, 3, 0, 1]
T_BANKS = (6, 7)
V_BANK = 5
ACC_BANKS = (4, 3, 2, 5)
HT_BANK, AUX_BANK = 1, 0

ALU = mybir.AluOpType
F32 = mybir.dt.float32
AX = mybir.AxisListType


def half_rows(n):
    return list(range(NB)) if n % 2 else list(range(NB - 2, -1, -1))


def half_cols(n, i):
    return list(range(i)) if n % 2 else list(range(NB - 1, i, -1))


def panel_number(n, i):
    return sum(len(half_rows(m)) for m in range(n)) + half_rows(n).index(i)


def ended(n, i):
    return NB * (n - 1) + (i if n % 2 else NB - 1 - i) + 1


def saved(n, i):
    return (NB - 1) * (n - 1) + (i if n % 2 == 0 else NB - 2 - i) + 1


def l_count(n, i):
    return NB * (n // 2) + i + 1


def graph_layers(nc, x, adj, W_u, diag_u, par_u, W_i, diag_i, par_i, ln_gamma, ln_beta, t, cheb_w, cheb_b,
                 sage_w, sage_b, out):
    with ExitStack() as ctx:
        def sb(name, shape):
            return ctx.enter_context(nc.sbuf_tensor(name, shape, F32))

        def sem(name):
            return ctx.enter_context(nc.semaphore(name))

        turned = nc.dram_tensor("turned", [NB, NB, P, Q * BW], F32).ap()

        pool = sb("pool", [P, SLOTS, Q, BW])
        X = sb("X", [P, NT, D])
        S = sb("S", [P, NT, 2 * D])
        part = sb("part", [P, NB, BW])
        yT = sb("yT", [P, 2, BW])
        hT = sb("hT", [D, 2, BW])
        g = sb("g", [P, 2, CH, D])
        tmp = sb("tmp", [P, CH, D])
        tmp2 = sb("tmp2", [P, CH, D])
        st1 = sb("st1", [P, CH])
        st2 = sb("st2", [P, CH])
        vT = yT
        minus_half = sb("minus_half", [P, CH])
        v_rows = sb("v_rows", [P, Q, D])
        rowsum = sb("rowsum", [P, NT])
        rs_part = sb("rs_part", [P, NB, Q])
        rdeg = sb("rdeg", [P, NT])
        ident = sb("ident", [P, P])
        fold = sb("fold", [P, D])
        w_ui = sb("w_ui", [D, 2, D])
        diag_rows = sb("diag_rows", [NT, P])
        pars = sb("pars", [P, 4])
        cpar = sb("cpar", [P, 2])
        cdiag = sb("cdiag", [P, NT])
        gamma8 = sb("gamma8", [P, D])
        beta = sb("beta", [P, D])
        b_cheb = sb("b_cheb", [P, D])
        b_sage = sb("b_sage", [P, D])
        wc = sb("wc", [P, 4, D])
        r_end = sb("r_end", [P, 2 * D])
        r_w3 = sb("r_w3", [P, D])
        r_aux = sb("r_aux", [D, D])
        r_sage = sb("r_sage", [P, D])
        r_sage_aux = sb("r_sage_aux", [D, 2, D])
        ps = ctx.enter_context(nc.psum_tensor("ps", [P, 8, BW], F32))

        x_in = [sem(f"x_in{m}") for m in range(NC)]
        small_in = sem("small_in")
        consts_step = sem("consts_step")
        consts = sem("consts")
        zeros = sem("zeros")
        a_in = [sem(f"a_in{s}") for s in range(A_SLOTS)]
        b_out = [sem(f"b_out{s}") for s in range(NB)]
        diag_turned = sem("diag_turned")
        h0_ready = sem("h0_ready")
        h0_turned = sem("h0_turned")
        h0_copied = sem("h0_copied")
        h0_w = sem("h0_w")
        e_ready = sem("e_ready")
        acc_zero = sem("acc_zero")
        t_ready = sem("t_ready")
        even_copied = sem("even_copied")
        odd_copied = sem("odd_copied")
        a_summed = sem("a_summed")
        rs_added = sem("rs_added")
        v_done = sem("v_done")
        vt_copied = sem("vt_copied")
        v_turned = sem("v_turned")
        v_ready = sem("v_ready")
        av_step = sem("av_step")
        gt_copied = sem("gt_copied")
        g_turned = sem("g_turned")
        g_ready = sem("g_ready")
        h1_ready = sem("h1_ready")
        blk_in = [sem(f"blk_in{s}") for s in range(SLOTS)]
        blk_used = sem("blk_used")
        acc_done = sem("acc_done")
        defer_done = sem("defer_done")
        part_saved = sem("part_saved")
        y_ready = sem("y_ready")
        y_upper = sem("y_upper")
        rows_ready = sem("rows_ready")
        rows_read = sem("rows_read")
        op_ready = sem("op_ready")
        ht_done = sem("ht_done")
        ht_copied = sem("ht_copied")
        aux_done = sem("aux_done")
        aux_read = sem("aux_read")
        fin_step = sem("fin_step")
        out_done = sem("out_done")
        dve_step = sem("dve_step")
        root_asked = sem("root_asked")
        root_done = sem("root_done")

        ring_list = [(n, i, j) for n in range(6) for i in half_rows(n) for j in half_cols(n, i)]
        ring_no = {b: k for k, b in enumerate(ring_list)}
        diag_list = [(n, i) for n in (1, 3, 5) for i in range(NB)]
        diag_no = {b: k for k, b in enumerate(diag_list)}

        def block(s):
            return pool[:, s, :, :]

        def flat(s):
            return pool[:, s, :, :].rearrange("p q i -> p (q i)")

        def lane(odd):
            return slice(D, 2 * D) if odd else slice(0, D)

        def turned_panel(J, n):
            if isinstance(J, int):
                return turned[J, n]
            return turned.rearrange("a n p f -> (a n p) f")[bass.ds(J * (NB * P) + n * P, P), :]

        def h1_chunk(j):
            return NC - j // 2

        block_ctx = ctx.enter_context(nc.Block())

        def store_out(sp, i):
            sp.wait_ge(fin_step, i + 1)
            dst = out[i * BW:(i + 1) * BW, :].rearrange("(q p) d -> p q d", p=P)
            sp.dma_start(dst, X[:, Q * i:Q * i + Q, :]).then_inc(out_done, 16)

        @block_ctx.sync
        def _(sp):
            def load_a(J, n, first):
                s = n % A_SLOTS
                if not (first and n < A_SLOTS):
                    sp.wait_ge(t_ready, 4 * (NB * J + n - A_SLOTS + 1))
                    sp.wait_ge(a_summed, NB * J + n - A_SLOTS + 1)
                src = adj[n * BW:(n + 1) * BW, bass.ts(J, BW)].rearrange("(q p) j -> p q j", p=P)
                sp.dma_start(block(NB + s), src).then_inc(a_in[s], 16)

            xr = x.rearrange("(t p) d -> p t d", p=P)
            sp.dma_start(X[:, 0:CH, :], xr[:, 0:CH, :]).then_inc(x_in[0], 16)
            sp.dma_start(w_ui[:, 0, :], W_u).then_inc(small_in, 16)
            sp.dma_start(w_ui[:, 1, :], W_i).then_inc(small_in, 16)
            sp.dma_start(diag_rows[0:NU // P, :], diag_u.rearrange("(t p) -> t p", p=P)).then_inc(small_in, 16)
            sp.dma_start(diag_rows[NU // P:, :], diag_i.rearrange("(t p) -> t p", p=P)).then_inc(small_in, 16)
            sp.dma_start(pars[:, 0:2], par_u.partition_broadcast(P)).then_inc(small_in, 16)
            sp.dma_start(pars[:, 2:4], par_i.partition_broadcast(P)).then_inc(small_in, 16)
            sp.dma_start(gamma8[:, :], ln_gamma.partition_broadcast(P)).then_inc(small_in, 16)
            sp.dma_start(beta[:, :], ln_beta.partition_broadcast(P)).then_inc(small_in, 16)
            sp.dma_start(b_cheb[:, :], cheb_b.partition_broadcast(P)).then_inc(small_in, 16)
            sp.dma_start(b_sage[:, :], sage_b.partition_broadcast(P)).then_inc(small_in, 16)
            for h in range(2):
                sp.dma_start(wc[lane(h), :, :], cheb_w.rearrange("k i o -> i k o")).then_inc(small_in, 16)
                sp.dma_start(r_sage[lane(h), :], sage_w[D:, :]).then_inc(small_in, 16)
            sp.dma_start(r_sage_aux[:, :, :], sage_w.rearrange("(k i) o -> i k o", k=2)).then_inc(small_in, 16)
            for n in range(NB):
                load_a(0, n, True)
                if n % 2 and n // 2 + 1 < NC:
                    m = n // 2 + 1
                    sp.dma_start(X[:, CH * m:CH * m + CH, :], xr[:, CH * m:CH * m + CH, :]).then_inc(x_in[m], 16)
            with sp.Fori(1, NB) as J:
                for n in range(NB):
                    load_a(J, n, False)

            for s in range(NB):
                sp.wait_ge(b_out[s], 16 * NB)
            ring_loads = {s: 0 for s in range(SLOTS)}
            for n in range(6):
                for i in half_rows(n):
                    for j in half_cols(n, i):
                        k = ring_no[n, i, j]
                        s = RING[k % len(RING)]
                        if k < 4:
                            sp.wait_ge(t_ready, 4 * NB * NB)
                            sp.wait_ge(a_summed, NB * NB)
                        elif k < len(RING):
                            sp.wait_ge(av_step, NC * (NB - 1) + (k - 4) // 2 + 1)
                        else:
                            sp.wait_ge(blk_used, k - len(RING) + 1)
                        sp.dma_start(flat(s), turned[j, i]).then_inc(blk_in[s], 16)
                    if n % 2:
                        k = diag_no[n, i]
                        if k >= 2:
                            m, r = diag_list[k - 2]
                            sp.wait_ge(acc_done if m == 5 else defer_done, l_count(m, r))
                        sp.dma_start(flat(DIAG[k % 2]), turned[i, i]).then_inc(blk_in[DIAG[k % 2]], 16)
                    if n == 5 and i:
                        store_out(sp, i - 1)
            store_out(sp, NB - 1)
            sp.wait_ge(out_done, 16 * NB)

        @block_ctx.gpsimd
        def _(pool_eng):
            steps = [0]

            def step(ins):
                steps[0] += 1
                ins.then_inc(consts_step, 1)
                pool_eng.wait_ge(consts_step, steps[0])

            nc.gpsimd.memset(part[:, 0, :], 0.0).then_inc(zeros, 1)
            step(nc.gpsimd.memset(ident[:, :], 0.0))
            step(nc.gpsimd.affine_select(out=ident[:, :], in_=ident[:, :], compare_op=ALU.not_equal, fill=1.0,
                                         base=0, pattern=[[-1, P]], channel_multiplier=1))
            nc.gpsimd.tensor_tensor(fold[:, :], ident[:, 0:D], ident[:, D:P], ALU.add).then_inc(consts, 1)
            pool_eng.wait_ge(consts, 1)
            pool_eng.wait_ge(small_in, 16 * 15)
            step(nc.gpsimd.tensor_tensor(r_end[lane(0), D:], wc[lane(0), 2, :], wc[lane(0), 2, :], ALU.add))
            step(nc.gpsimd.tensor_tensor(r_end[lane(1), D:], wc[lane(1), 1, :], wc[lane(1), 3, :], ALU.subtract))
            step(nc.gpsimd.tensor_tensor(r_w3[lane(1), :], wc[lane(1), 3, :], wc[lane(1), 3, :], ALU.add))
            step(nc.gpsimd.tensor_tensor(r_aux[:, :], wc[lane(0), 0, :], wc[lane(0), 2, :], ALU.subtract))
            step(nc.gpsimd.memset(minus_half[:, :], -0.5))
            nc.gpsimd.tensor_copy(r_end[:, 0:D], fold[:, :]).then_inc(consts, 1)

            for k in range(3 * NC + 3 * NB):
                m2 = st2[:, 0:CH if k < 3 * NC else Q]
                pool_eng.wait_ge(root_asked, k + 1)
                nc.gpsimd.tensor_tensor(m2, m2, minus_half[:, 0:m2.shape[1]], ALU.pow).then_inc(root_done, 1)

        @block_ctx.tensor
        def _(pe):
            mm = nc.tensor.matmul

            def turn_h0(m):
                pe.wait_ge(h0_ready, m + 1)
                for k in range(CH):
                    ins = nc.tensor.transpose(ps[0:D, k // Q, (k % Q) * P:(k % Q + 1) * P],
                                              S[:, CH * m + k, D:], ident[:, :])
                ins.then_inc(h0_turned, 1)
                pe.wait_ge(h0_copied, m + 1)
                if m:
                    pe.wait_ge(e_ready, m)
                for k in range(CH):
                    ins = mm(ps[:, 2, D * k:D * k + D], hT[:, k // Q, (k % Q) * P:(k % Q + 1) * P],
                             w_ui[:, int(m >= NU // (CH * P)), :], start=True, stop=True)
                ins.then_inc(h0_w, 1)

            def turn_v(J):
                pe.wait_ge(even_copied, NB * 2 * J)
                pe.wait_ge(odd_copied, NB * 2 * J)
                for q in range(Q):
                    ins = mm(ps[:, T_BANKS[0], D * q:D * q + D], vT[:, 0, q * P:(q + 1) * P], fold[:, :],
                             start=True, stop=True)
                ins.then_inc(v_turned, 1)
                pe.wait_ge(v_ready, J)

            def add_av(m):
                for q in range(Q):
                    for n in (2 * m, 2 * m + 1):
                        ins = mm(ps[lane(n % 2), m, :], v_rows[:, q, :], pool[:, n, q, :],
                                 start=False, stop=False, skip_group_check=True)
                ins.then_inc(av_step, 1)

            def panel(J, first):
                for m in range(NC):
                    if first:
                        turn_h0(m)
                        pe.wait_ge(e_ready, m + 1)
                    elif m == 0:
                        pe.wait_ge(vt_copied, J)
                    for n in (2 * m, 2 * m + 1):
                        pe.wait_ge(a_in[n % A_SLOTS], 16 * (2 * J + n // A_SLOTS + 1))
                        for q in range(Q):
                            ins = mm(ps[lane(q % 2), V_BANK, :], S[:, Q * n + q, 0:D], pool[:, NB + n % A_SLOTS, q, :],
                                     start=(n == 0 and q < 2), stop=(n == NB - 1 and q >= 2), skip_group_check=True)
                    if m == NC - 1:
                        ins.then_inc(v_done, 1)
                    if not first:
                        if m == 0:
                            turn_v(J)
                        add_av(m)
                    for n in (2 * m, 2 * m + 1):
                        for qj in range(Q):
                            k = Q * n + qj
                            if k >= 2:
                                pe.wait_ge((even_copied, odd_copied)[k % 2], 2 * NB * J + k // 2)
                            for qi in range(Q):
                                ins = nc.tensor.transpose(ps[:, T_BANKS[k % 2], qi * P:(qi + 1) * P],
                                                          pool[:, NB + n % A_SLOTS, qi, qj * P:(qj + 1) * P],
                                                          ident[:, :])
                            ins.then_inc(t_ready, 1)

            pe.wait_ge(consts, 1)
            pe.wait_ge(small_in, 16 * 15)
            nc.tensor.transpose(ps[:, 3, 0:NT], diag_rows[:, :], ident[0:NT, 0:NT]).then_inc(diag_turned, 1)
            panel(0, True)
            pe.wait_ge(zeros, 1)
            for m in range(NC):
                for h in range(2):
                    mm(ps[lane(h), m, :], part[:, 0, 0:D], part[:, 0, :], start=True, stop=False, skip_group_check=True)
            with pe.Fori(1, NB) as J:
                panel(J, False)
            pe.wait_ge(vt_copied, NB)
            turn_v(NB)

            def turn_av(k):
                pe.wait_ge(gt_copied, k + 1)
                if k >= 2:
                    pe.wait_ge(g_ready, k - 1)
                for q in range(Q):
                    ins = nc.tensor.transpose(ps[:, T_BANKS[k % 2], q * P:(q + 1) * P],
                                              yT[:, k % 2, q * P:(q + 1) * P], ident[:, :])
                ins.then_inc(g_turned, 1)

            for k in range(NC):
                add_av(NC - 1 - k)
                if k:
                    turn_av(k - 1)
            turn_av(NC - 1)

            def wait_block(n, i, j):
                k = ring_no[n, i, j]
                pe.wait_ge(blk_in[RING[k % len(RING)]], 16 * (k // len(RING) + 1))
                return pool[:, RING[k % len(RING)], :, :]

            def wait_diag(n, i):
                k = diag_no[n, i]
                pe.wait_ge(blk_in[DIAG[k % 2]], 16 * (k // 2 + 1))
                return pool[:, DIAG[k % 2], :, :]

            def wait_bank(n, i):
                k = panel_number(n, i)
                if k < 3:
                    pe.wait_ge(gt_copied, k + 1)
                if k >= 4:
                    m, r = [(a, b) for a in range(6) for b in half_rows(a)][k - 4]
                    if m:
                        pe.wait_ge(y_ready, ended(m, r))
                    if m == 5:
                        pe.wait_ge(y_upper, NB - 1 + r + 1)
                    elif m % 2 and r == NB - 1:
                        pe.wait_ge(y_ready, ended(m + 1, r))
                    else:
                        pe.wait_ge(part_saved, saved(m + 1, r))
                return ACC_BANKS[k % 4]

            def off_diagonal(n, i, j, bank, start, stop):
                b = wait_block(n, i, j)
                if n == 0:
                    pe.wait_ge(h1_ready, h1_chunk(j))
                else:
                    pe.wait_ge(op_ready, ended(min(n, 4), j))
                for q in range(Q):
                    if n in (0, 5):
                        ins = mm(ps[lane(q % 2), bank, :], S[:, Q * j + q, 0:D], b[:, q, :],
                                 start=start and q < 2, stop=stop and q >= 2, skip_group_check=True)
                    else:
                        ins = mm(ps[:, bank, :], S[:, Q * j + q, :], b[:, q, :],
                                 start=start and q == 0, stop=stop and q == Q - 1, skip_group_check=True)
                return ins

            def on_diagonal(n, i):
                own = lane(n % 2 == 0)
                other = lane(n % 2)
                ins = dins = None
                if i < NB:
                    b = wait_diag(n, i)
                    pe.wait_ge(op_ready, ended(n - 1, i)) if n > 1 else pe.wait_ge(h1_ready, h1_chunk(i))
                    bank = ACC_BANKS[panel_number(n, i) % 4]
                if n < 5 and i > 0:
                    d = wait_diag(n, i - 1)
                    pe.wait_ge(op_ready, ended(n, i - 1))
                    dbank = ACC_BANKS[panel_number(n, i - 1) % 4]
                for q in range(Q):
                    if i < NB and n == 5:
                        ins = mm(ps[lane(q % 2), bank, :], S[:, Q * i + q, own], b[:, q, :],
                                 start=(i == 0 and q < 2), stop=(q >= 2), skip_group_check=True)
                    elif i < NB:
                        ins = mm(ps[own, bank, :], S[:, Q * i + q, own], b[:, q, :],
                                 start=(i == 0 and q == 0), stop=(q == Q - 1), skip_group_check=True)
                    if q == Q - 1 and ins is not None:
                        ins.then_inc(acc_done, 1)
                    if n < 5 and i > 0:
                        dins = mm(ps[other, dbank, :], S[:, Q * (i - 1) + q, other], d[:, q, :],
                                  start=(i == 1 and q == 0), stop=(q == Q - 1), skip_group_check=True)
                if dins is not None:
                    dins.then_inc(defer_done, 1)

            def end_rows(n, i):
                c = ended(n, i)
                pe.wait_ge(y_ready, c)
                if n == 1 and i < NB - 1:
                    pe.wait_ge(y_upper, i + 1)
                if n == 5:
                    pe.wait_ge(y_upper, NB - 1 + i + 1)
                if c > 2:
                    pe.wait_ge(rows_read, c - 2)
                sl, rhs = {
                    1: (slice(0, P) if i < NB - 1 else lane(0), fold[:, :]),
                    2: (lane(1), r_end[:, :]),
                    3: (lane(0), r_end[:, :]),
                    4: (lane(1), r_w3[:, :]),
                    5: (slice(0, P), r_sage[:, :]),
                }[n]
                w = rhs.shape[1]
                for q in range(Q):
                    ins = mm(ps[:, T_BANKS[c % 2], P * q:P * q + w], yT[sl, c % 2, q * P:(q + 1) * P], rhs[sl, :],
                             start=True, stop=True)
                ins.then_inc(rows_ready, 1)

            def aux_turn(u):
                i = u % NB
                if u:
                    pe.wait_ge(ht_copied, u)
                pe.wait_ge(op_ready, ended(1, i) if u < NB else ended(4, i))
                src = lane(u < NB)
                for q in range(Q):
                    ins = nc.tensor.transpose(ps[0:D, HT_BANK, q * P:(q + 1) * P], S[:, Q * i + q, src], ident[:, :])
                ins.then_inc(ht_done, 1)

            def aux_mul(u):
                pe.wait_ge(ht_copied, u + 1)
                if u:
                    pe.wait_ge(aux_read, u)
                rhs = r_aux[:, :] if u < NB else r_sage_aux[:, :, :].rearrange("p k d -> p (k d)")
                w = rhs.shape[1]
                for q in range(Q):
                    ins = mm(ps[:, AUX_BANK, P * q:P * q + w], hT[:, u % 2, q * P:(q + 1) * P], rhs,
                             start=True, stop=True)
                ins.then_inc(aux_done, 1)

            pe.wait_ge(consts, 2)
            for n in range(6):
                pending = None
                if n in (2, 4):
                    end_rows(n, NB - 1)

                def flush(i, n=n):
                    end_rows(n, i)
                    if n == 1:
                        if i >= 2:
                            aux_mul(i - 2)
                        if i >= 1:
                            aux_turn(i - 1)

                for i in half_rows(n):
                    bank = wait_bank(n, i)
                    cols = half_cols(n, i)
                    for idx, j in enumerate(cols):
                        if n and pending is not None and j == pending:
                            flush(pending)
                            pending = None
                        ins = off_diagonal(n, i, j, bank, idx == 0, n % 2 == 0 and idx == len(cols) - 1)
                        ins.then_inc(blk_used, 1)
                        if n and pending is not None and idx == 0:
                            flush(pending)
                            pending = None
                        if n == 5 and idx == 0:
                            aux_turn(NB + i)
                    if n % 2:
                        if n == 5 and i == 0:
                            aux_turn(NB)
                        on_diagonal(n, i)
                    if n == 5:
                        aux_mul(NB + i)
                    pending = i
                if n:
                    flush(pending)
                if n == 1:
                    aux_mul(NB - 2)
                if n in (1, 3):
                    on_diagonal(n, NB)
                if n == 1:
                    aux_turn(NB - 1)
                    aux_mul(NB - 1)

        @block_ctx.scalar
        def _(act):
            def panel(J, first):
                for m in range(NC):
                    if first:
                        act.wait_ge(h0_turned, m + 1)
                        if m:
                            act.wait_ge(h0_w, m)
                        nc.scalar.copy(hT[:, :, :], ps[0:D, 0:2, :]).then_inc(h0_copied, 1)
                    for n in (2 * m, 2 * m + 1):
                        if not first:
                            act.wait_ge(av_step, NC * (J - 1) + m + 1)
                            act.wait_ge(b_out[n], 16 * J)
                        for qj in (1, 3):
                            act.wait_ge(t_ready, Q * NB * J + Q * n + qj + 1)
                            nc.scalar.copy(pool[:, n, qj, :], ps[:, T_BANKS[1], :]).then_inc(odd_copied, 1)
                        act.wait_ge(even_copied, 2 * NB * J + 2 * n + 2)
                        act.wait_ge(odd_copied, 2 * NB * J + 2 * n + 2)
                        act.dma_start(turned_panel(J, n), flat(n)).then_inc(b_out[n], 16)
                act.wait_ge(v_done, J + 1)
                nc.scalar.copy(vT[:, 0, :], ps[:, V_BANK, :]).then_inc(vt_copied, 1)

            panel(0, True)
            with act.Fori(1, NB) as J:
                panel(J, False)

            def copy_gt(k):
                act.wait_ge(av_step, NC * (NB - 1) + k + 1)
                if k >= 2:
                    act.wait_ge(g_turned, k - 1)
                nc.scalar.copy(yT[:, k % 2, :], ps[:, NC - 1 - k, :]).then_inc(gt_copied, 1)

            def copy_g(k):
                act.wait_ge(g_turned, k + 1)
                if k >= 2:
                    act.wait_ge(h1_ready, k - 1)
                nc.scalar.copy(g[:, k % 2, :, :].rearrange("p (b q) d -> p b q d", b=2),
                               ps[:, T_BANKS[k % 2], :].rearrange("p (q b d) -> p b q d", q=Q, b=2)).then_inc(g_ready, 1)

            for k in range(NC):
                copy_gt(k)
                if k:
                    copy_g(k - 1)
            copy_g(NC - 1)

            def save(n, i):
                m = n - 1
                if m % 2:
                    act.wait_ge(defer_done, l_count(m, i))
                else:
                    act.wait_ge(blk_used, ring_no[m, i, i + 1] + 1)
                if n == 2:
                    act.wait_ge(y_upper, i + 1)
                sl = slice(0, P) if n == 1 else lane(n % 2 == 0)
                nc.scalar.copy(part[sl, i, :], ps[sl, ACC_BANKS[panel_number(m, i) % 4], :]).then_inc(part_saved, 1)

            def upper(n, i):
                c = ended(n, i)
                if c > 2:
                    act.wait_ge(rows_ready, c - 2)
                if n == 1:
                    act.wait_ge(part_saved, saved(1, i))
                    src = part[lane(1), i, :]
                else:
                    act.wait_ge(acc_done, l_count(5, i))
                    src = ps[lane(1), ACC_BANKS[panel_number(5, i) % 4], :]
                nc.scalar.copy(yT[lane(1), c % 2, :], src).then_inc(y_upper, 1)

            def copy_ht(u):
                act.wait_ge(ht_done, u + 1)
                if u >= 2:
                    act.wait_ge(aux_done, u - 1)
                nc.scalar.copy(hT[:, u % 2, :], ps[0:D, HT_BANK, :]).then_inc(ht_copied, 1)

            for i in half_rows(0):
                save(1, i)
            for i in range(NB + 1):
                if 1 <= i < NB:
                    upper(1, i - 1)
                if i >= 2:
                    copy_ht(i - 2)
                if 1 <= i < NB:
                    save(2, i - 1)
            copy_ht(NB - 1)
            for i in half_rows(2):
                save(3, i)
            for i in range(NB - 1):
                save(4, i)
            for i in half_rows(4):
                save(5, i)
            for i in range(NB):
                if i:
                    upper(5, i - 1)
                copy_ht(NB + i)
                act.wait_ge(aux_done, NB + i + 1)
                if i >= 2:
                    act.wait_ge(fin_step, i - 1)
                nc.scalar.copy(g[:, i % 2, :, :].rearrange("p t d -> p (t d)"), ps[:, AUX_BANK, :]).then_inc(aux_read, 1)
            upper(5, NB - 1)

        @block_ctx.vector
        def _(dve):
            vec = nc.vector
            steps = [0]

            def step(ins):
                steps[0] += 1
                ins.then_inc(dve_step, 1)
                dve.wait_ge(dve_step, steps[0])

            roots = [0]

            def wait_root():
                roots[0] += 1
                dve.wait_ge(root_done, roots[0])

            def cols(stat, t):
                return stat.unsqueeze(2).to_broadcast([P, t, D])

            def rows(vecs, t):
                return vecs.unsqueeze(1).to_broadcast([P, t, D])

            def normalise(src, t):
                a, b, m1, m2 = tmp[:, 0:t, :], tmp2[:, 0:t, :], st1[:, 0:t], st2[:, 0:t]
                step(vec.tensor_reduce(m1, src, AX.X, ALU.add))
                step(vec.scalar_tensor_tensor(out=a, in0=cols(m1, t), scalar=-1.0 / D, in1=src, op0=ALU.mult, op1=ALU.add))
                step(vec.tensor_tensor(b, a, a, ALU.mult))
                step(vec.tensor_reduce(m2, b, AX.X, ALU.add))
                vec.tensor_scalar(m2, m2, D * EPS, None, ALU.add).then_inc(root_asked, 1)
                wait_root()
                step(vec.tensor_tensor(a, a, cols(m2, t), ALU.mult))
                return a

            def relu_norm(src, dst, t):
                return vec.tensor_scalar(dst, normalise(src, t), 8.0, 0.0, ALU.mult, ALU.max)

            def make_e(m):
                c = slice(CH * m, CH * m + CH)
                dve.wait_ge(x_in[m], 16)
                relu_norm(X[:, c, :], S[:, c, D:], CH).then_inc(h0_ready, 1)
                dve.wait_ge(h0_ready, m + 1)
                step(vec.tensor_tensor(X[:, c, :], X[:, c, :], S[:, c, D:], ALU.add))
                if m == 0:
                    dve.wait_ge(small_in, 16 * 15)
                    step(vec.tensor_tensor(cpar[:, :], pars[:, 0:4:2], pars[:, 1:4:2], ALU.mult))
                    dve.wait_ge(diag_turned, 1)
                    nu = NU // P
                    step(vec.tensor_scalar(cdiag[:, 0:nu], ps[:, 3, 0:nu], cpar[:, 0:1], None, ALU.mult))
                    step(vec.tensor_scalar(cdiag[:, nu:], ps[:, 3, nu:NT], cpar[:, 1:2], None, ALU.mult))
                    step(vec.tensor_scalar(gamma8[:, :], gamma8[:, :], 8.0, None, ALU.mult))
                step(vec.tensor_tensor(X[:, c, :], X[:, c, :], rows(beta[:, :], CH), ALU.add))
                dve.wait_ge(h0_w, m + 1)
                step(vec.tensor_tensor(tmp[:, :, :], ps[:, 2, :].rearrange("p (t d) -> p t d", t=CH),
                                       cols(cdiag[:, c], CH), ALU.mult))
                vec.tensor_tensor(S[:, c, 0:D], tmp[:, :, :], S[:, c, D:], ALU.add).then_inc(e_ready, 1)
                dve.wait_ge(e_ready, m + 1)

            def panel(J, first):
                if not first:
                    copy_v(J)
                for m in range(NC):
                    if first and m == 0:
                        make_e(0)
                    for n in (2 * m, 2 * m + 1):
                        if not first:
                            dve.wait_ge(av_step, NC * (J - 1) + m + 1)
                            dve.wait_ge(b_out[n], 16 * J)
                        for qj in (0, 2):
                            dve.wait_ge(t_ready, Q * NB * J + Q * n + qj + 1)
                            vec.tensor_copy(pool[:, n, qj, :], ps[:, T_BANKS[0], :]).then_inc(even_copied, 1)
                        dve.wait_ge(a_in[n % A_SLOTS], 16 * (2 * J + n // A_SLOTS + 1))
                        if not first:
                            dve.wait_ge(rs_added, NB * (J - 1) + n + 1)
                        vec.tensor_reduce(rs_part[:, n, :], block(NB + n % A_SLOTS), AX.X, ALU.add).then_inc(a_summed, 1)
                        dve.wait_ge(a_summed, NB * J + n + 1)
                        r = rowsum[:, Q * n:Q * n + Q]
                        vec.tensor_tensor(r, r, rs_part[:, n, :], ALU.add).then_inc(rs_added, 1)
                    if first and m < NC - 1:
                        make_e(m + 1)

            def copy_v(J):
                dve.wait_ge(v_turned, J)
                vec.tensor_copy(v_rows[:, :, :].rearrange("p q d -> p (q d)"), ps[:, T_BANKS[0], 0:Q * D]).then_inc(v_ready, 1)

            step(vec.memset(rowsum[:, :], 0.0))
            panel(0, True)
            with dve.Fori(1, NB) as J:
                panel(J, False)
            copy_v(NB)

            dve.wait_ge(rs_added, NB * NB)
            step(vec.tensor_scalar(rdeg[:, :], rowsum[:, :], 1.0, 1.0, ALU.add, ALU.max))
            step(vec.reciprocal(rdeg[:, :], rdeg[:, :]))

            for k in range(NC):
                c = slice(CH * (NC - 1 - k), CH * (NC - k))
                dve.wait_ge(g_ready, k + 1)
                a = normalise(g[:, k % 2, :, :], CH)
                step(vec.tensor_tensor(a, a, rows(gamma8[:, :], CH), ALU.mult))
                step(vec.tensor_tensor(X[:, c, :], X[:, c, :], a, ALU.add))
                relu_norm(X[:, c, :], S[:, c, 0:D], CH).then_inc(h1_ready, 1)
                dve.wait_ge(h1_ready, k + 1)

            def end_sum(n, i):
                c = ended(n, i)
                h = lane(n % 2 == 0)
                m = n if n % 2 or i < NB - 1 else n - 1
                if m % 2 == 0:
                    dve.wait_ge(blk_used, ring_no[n, i, i + 1] + 1)
                elif m == n:
                    dve.wait_ge(acc_done, l_count(n, i))
                else:
                    dve.wait_ge(defer_done, l_count(m, i))
                if c > 2:
                    dve.wait_ge(rows_ready, c - 2)
                acc = ps[h, ACC_BANKS[panel_number(m, i) % 4], :]
                if i < NB - 1:
                    dve.wait_ge(part_saved, saved(n, i))
                    vec.tensor_tensor(yT[h, c % 2, :], acc, part[h, i, :], ALU.add).then_inc(y_ready, 1)
                else:
                    vec.tensor_copy(yT[h, c % 2, :], acc).then_inc(y_ready, 1)

            def end_layer(n, i):
                c = ended(n, i)
                ti = slice(Q * i, Q * i + Q)
                x_i, odd, even = X[:, ti, :], S[:, ti, 0:D], S[:, ti, D:]
                r = ps[:, T_BANKS[c % 2], :].rearrange("p (q k d) -> p q k d", q=Q, k=2)
                r0, r1 = r[:, :, 0, :], r[:, :, 1, :]
                a, b, m1 = tmp[:, 0:Q, :], tmp2[:, 0:Q, :], st1[:, 0:Q]
                dve.wait_ge(rows_ready, c)

                def read(ins):
                    ins.then_inc(rows_read, 1)
                    dve.wait_ge(rows_read, c)

                if n == 1:
                    read(vec.tensor_tensor(a, r0, odd, ALU.mult))
                    step(vec.tensor_reduce(m1, a, AX.X, ALU.add))
                    step(vec.tensor_scalar(m1, m1, -0.01, 1.0, ALU.mult, ALU.add))
                    step(vec.scalar_tensor_tensor(out=a, in0=odd, scalar=-0.1, in1=x_i, op0=ALU.mult, op1=ALU.add))
                    step(vec.tensor_tensor(x_i, a, cols(m1, Q), ALU.add))
                    relu_norm(x_i, even, Q).then_inc(op_ready, 1)
                elif n == 2:
                    vec.tensor_copy(odd, r0).then_inc(op_ready, 1)
                    read(vec.tensor_tensor(x_i, x_i, r1, ALU.add))
                elif n == 3:
                    vec.scalar_tensor_tensor(out=even, in0=r0, scalar=2.0, in1=even, op0=ALU.mult,
                                             op1=ALU.subtract).then_inc(op_ready, 1)
                    read(vec.tensor_tensor(x_i, x_i, r1, ALU.add))
                elif n == 4:
                    read(vec.tensor_tensor(x_i, x_i, r0, ALU.add))
                    relu_norm(x_i, odd, Q).then_inc(op_ready, 1)
                else:
                    dve.wait_ge(aux_read, NB + i + 1)
                    gi = g[:, i % 2, :, :].rearrange("p (q k) d -> p q k d", k=2)
                    read(vec.tensor_tensor(a, r0, gi[:, :, 1, :], ALU.add))
                    step(vec.tensor_tensor(a, a, cols(rdeg[:, ti], Q), ALU.mult))
                    step(vec.tensor_tensor(a, a, gi[:, :, 0, :], ALU.add))
                    step(vec.tensor_tensor(a, a, rows(b_sage[:, :], Q), ALU.add))
                    step(vec.tensor_scalar(a, a, 0.0, None, ALU.max))
                    step(vec.tensor_tensor(b, a, a, ALU.mult))
                    step(vec.tensor_reduce(m1, b, AX.X, ALU.add))
                    vec.tensor_scalar(st2[:, 0:Q], m1, 1e-24, None, ALU.max).then_inc(root_asked, 1)
                    wait_root()
                    step(vec.tensor_tensor(a, a, cols(st2[:, 0:Q], Q), ALU.mult))
                    vec.tensor_tensor(x_i, x_i, a, ALU.add).then_inc(fin_step, 1)
                    dve.wait_ge(fin_step, i + 1)
                if n < 5:
                    dve.wait_ge(op_ready, c)

            def add_aux(i):
                x_i = X[:, Q * i:Q * i + Q, :]
                dve.wait_ge(aux_done, i + 1)
                ps_i = ps[:, AUX_BANK, :].rearrange("p (q k) -> p q k", q=Q)[:, :, 0:D]
                vec.tensor_tensor(x_i, x_i, ps_i, ALU.add).then_inc(aux_read, 1)
                dve.wait_ge(aux_read, i + 1)
                step(vec.tensor_tensor(x_i, x_i, rows(b_cheb[:, :], Q), ALU.add))

            for n in range(1, 6):
                if n % 2 == 0:
                    end_sum(n, NB - 1)
                    if n == 2:
                        add_aux(NB - 2)
                        add_aux(NB - 1)
                    end_layer(n, NB - 1)
                for i in half_rows(n):
                    end_sum(n, i)
                    end_layer(n, i)
                    if n == 1 and i >= 2:
                        add_aux(i - 2)


_INS = ["x", "adj", "L0_gnn_W_u", "L0_gnn_diag_u", "L0_gnn_par_u", "L0_gnn_W_i", "L0_gnn_diag_i", "L0_gnn_par_i",
        "L0_gnn_ln_gamma", "L0_gnn_ln_beta", "L1_gnn_t", "L2_gnn_weight", "L2_gnn_bias", "L3_gnn_W", "L3_gnn_b"]


def kernel(**inputs):
    import numpy as _np
    import concourse.bacc as _bacc
    from concourse import mybir as _mybir
    from concourse.bass_utils import run_bass_kernel_spmd as _run

    nc = _bacc.Bacc("TRN2", target_bir_lowering=False, num_devices=1)
    arrays, args = {}, []
    for name in _INS:
        a = _np.ascontiguousarray(inputs[name])
        arrays[f"in_{name}"] = a
        args.append(nc.dram_tensor(f"in_{name}", a.shape, _mybir.dt.from_np(a.dtype), kind="ExternalInput").ap())
    args.append(nc.dram_tensor("out", (N, D), F32, kind="ExternalOutput").ap())
    graph_layers(nc, *args)
    r = _run(nc, [arrays], core_ids=[0])
    return r.results[0]["out"]
```

```python
from contextlib import ExitStack

import concourse.bass as bass
from concourse import mybir

P = 128
D = 64
BW = 512
Q = BW // P
N = 5120
NB = N // BW
NT = N // P
CH = 2 * Q
NC = NT // CH
NU = 2048
EPS = 1e-5
A_SLOTS = 5
DIAG = [A_SLOTS + NB - 1, A_SLOTS + NB]
SLOTS = A_SLOTS + NB + 1
ORDER = [8, 9, 6, 7, 4, 5, 2, 3, 0, 1]
RING = [NB, NB + 1, NB + 2, NB + 3, 8, 9, 6, 7, 4, 5, 2, 3, 0, 1]
T_BANKS = (6, 7)
V_BANK = 5
ACC_BANKS = (4, 3, 2, 5)
HT_BANK, AUX_BANK = 1, 0

ALU = mybir.AluOpType
F32 = mybir.dt.float32
AX = mybir.AxisListType


def half_rows(n):
    return list(range(NB)) if n % 2 else list(range(NB - 2, -1, -1))


def half_cols(n, i):
    return list(range(i)) if n % 2 else list(range(NB - 1, i, -1))


def panel_number(n, i):
    return sum(len(half_rows(m)) for m in range(n)) + half_rows(n).index(i)


def ended(n, i):
    return NB * (n - 1) + (i if n % 2 else NB - 1 - i) + 1


def saved(n, i):
    return (NB - 1) * (n - 1) + (i if n % 2 == 0 else NB - 2 - i) + 1


def l_count(n, i):
    return NB * (n // 2) + i + 1


def graph_layers(nc, x, adj, W_u, diag_u, par_u, W_i, diag_i, par_i, ln_gamma, ln_beta, t, cheb_w, cheb_b,
                 sage_w, sage_b, out):
    with ExitStack() as ctx:
        def sb(name, shape):
            return ctx.enter_context(nc.sbuf_tensor(name, shape, F32))

        def sem(name):
            return ctx.enter_context(nc.semaphore(name))

        turned = nc.dram_tensor("turned", [NB, NB, P, Q * BW], F32).ap()

        pool = sb("pool", [P, SLOTS, Q, BW])
        X = sb("X", [P, NT, D])
        S = sb("S", [P, NT, 2 * D])
        part = sb("part", [P, NB, BW])
        yT = sb("yT", [P, 2, BW])
        hT = sb("hT", [D, 2, BW])
        g = sb("g", [P, 2, CH, D])
        tmp = sb("tmp", [P, CH, D])
        tmp2 = sb("tmp2", [P, CH, D])
        st1 = sb("st1", [P, CH])
        st2 = sb("st2", [P, CH])
        vT = yT
        minus_half = sb("minus_half", [P, CH])
        v_rows = sb("v_rows", [P, Q, D])
        rowsum = sb("rowsum", [P, NT])
        rs_part = sb("rs_part", [P, NB, Q])
        rdeg = sb("rdeg", [P, NT])
        ident = sb("ident", [P, P])
        fold = sb("fold", [P, D])
        w_ui = sb("w_ui", [D, 2, D])
        diag_rows = sb("diag_rows", [NT, P])
        pars = sb("pars", [P, 4])
        cpar = sb("cpar", [P, 2])
        cdiag = sb("cdiag", [P, NT])
        gamma8 = sb("gamma8", [P, D])
        beta = sb("beta", [P, D])
        b_cheb = sb("b_cheb", [P, D])
        b_sage = sb("b_sage", [P, D])
        wc = sb("wc", [P, 4, D])
        r_end = sb("r_end", [P, 2 * D])
        r_w3 = sb("r_w3", [P, D])
        r_aux = sb("r_aux", [D, D])
        r_sage = sb("r_sage", [P, D])
        r_sage_aux = sb("r_sage_aux", [D, 2, D])
        ps = ctx.enter_context(nc.psum_tensor("ps", [P, 8, BW], F32))

        x_in = [sem(f"x_in{m}") for m in range(NC)]
        small_in = sem("small_in")
        consts_step = sem("consts_step")
        consts = sem("consts")
        zeros = sem("zeros")
        a_in = [sem(f"a_in{s}") for s in range(A_SLOTS)]
        b_out = [sem(f"b_out{s}") for s in range(NB)]
        diag_turned = sem("diag_turned")
        h0_ready = sem("h0_ready")
        h0_turned = sem("h0_turned")
        h0_copied = sem("h0_copied")
        h0_w = sem("h0_w")
        e_ready = sem("e_ready")
        acc_zero = sem("acc_zero")
        t_ready = sem("t_ready")
        even_copied = sem("even_copied")
        odd_copied = sem("odd_copied")
        a_summed = sem("a_summed")
        rs_added = sem("rs_added")
        v_done = sem("v_done")
        vt_copied = sem("vt_copied")
        v_turned = sem("v_turned")
        v_ready = sem("v_ready")
        av_step = sem("av_step")
        gt_copied = sem("gt_copied")
        g_turned = sem("g_turned")
        g_ready = sem("g_ready")
        h1_ready = sem("h1_ready")
        blk_in = [sem(f"blk_in{s}") for s in range(SLOTS)]
        blk_used = sem("blk_used")
        acc_done = sem("acc_done")
        defer_done = sem("defer_done")
        part_saved = sem("part_saved")
        y_ready = sem("y_ready")
        y_upper = sem("y_upper")
        rows_ready = sem("rows_ready")
        rows_read = sem("rows_read")
        op_ready = sem("op_ready")
        ht_done = sem("ht_done")
        ht_copied = sem("ht_copied")
        aux_done = sem("aux_done")
        aux_read = sem("aux_read")
        fin_step = sem("fin_step")
        out_done = sem("out_done")
        dve_step = sem("dve_step")
        root_asked = sem("root_asked")
        root_done = sem("root_done")

        ring_list = [(n, i, j) for n in range(6) for i in half_rows(n) for j in half_cols(n, i)]
        ring_no = {b: k for k, b in enumerate(ring_list)}
        diag_list = [(n, i) for n in (1, 3, 5) for i in range(NB)]
        diag_no = {b: k for k, b in enumerate(diag_list)}

        def block(s):
            return pool[:, s, :, :]

        def flat(s):
            return pool[:, s, :, :].rearrange("p q i -> p (q i)")

        def lane(odd):
            return slice(D, 2 * D) if odd else slice(0, D)

        def turned_panel(J, n):
            if isinstance(J, int):
                return turned[J, n]
            return turned.rearrange("a n p f -> (a n p) f")[bass.ds(J * (NB * P) + n * P, P), :]

        def h1_chunk(j):
            return NC - j // 2

        block_ctx = ctx.enter_context(nc.Block())

        def store_out(sp, i):
            sp.wait_ge(fin_step, i + 1)
            dst = out[i * BW:(i + 1) * BW, :].rearrange("(q p) d -> p q d", p=P)
            sp.dma_start(dst, X[:, Q * i:Q * i + Q, :]).then_inc(out_done, 16)

        @block_ctx.sync
        def _(sp):
            def load_a(J, k, first, j=0):
                s, n = k % A_SLOTS, ORDER[k]
                rows = adj[n * BW:(n + 1) * BW, 0 if first else BW:]
                src = rows[:, bass.ts(J if first else j, BW)].rearrange("(q p) j -> p q j", p=P)
                if not (first and k < A_SLOTS):
                    sp.wait_ge(t_ready, Q * (NB * J + k - A_SLOTS + 1))
                    sp.wait_ge(a_summed, NB * J + k - A_SLOTS + 1)
                sp.dma_start(block(NB + s), src).then_inc(a_in[s], 16)

            def load_x(m):
                xr = x.rearrange("(t p) d -> p t d", p=P)
                sp.dma_start(X[:, CH * m:CH * m + CH, :], xr[:, CH * m:CH * m + CH, :]).then_inc(x_in[m], 16)

            load_x(NC - 1)
            sp.dma_start(w_ui[:, 0, :], W_u).then_inc(small_in, 16)
            sp.dma_start(w_ui[:, 1, :], W_i).then_inc(small_in, 16)
            sp.dma_start(diag_rows[0:NU // P, :], diag_u.rearrange("(t p) -> t p", p=P)).then_inc(small_in, 16)
            sp.dma_start(diag_rows[NU // P:, :], diag_i.rearrange("(t p) -> t p", p=P)).then_inc(small_in, 16)
            sp.dma_start(pars[:, 0:2], par_u.partition_broadcast(P)).then_inc(small_in, 16)
            sp.dma_start(pars[:, 2:4], par_i.partition_broadcast(P)).then_inc(small_in, 16)
            sp.dma_start(gamma8[:, :], ln_gamma.partition_broadcast(P)).then_inc(small_in, 16)
            sp.dma_start(beta[:, :], ln_beta.partition_broadcast(P)).then_inc(small_in, 16)
            sp.dma_start(b_cheb[:, :], cheb_b.partition_broadcast(P)).then_inc(small_in, 16)
            sp.dma_start(b_sage[:, :], sage_b.partition_broadcast(P)).then_inc(small_in, 16)
            for h in range(2):
                sp.dma_start(wc[lane(h), :, :], cheb_w.rearrange("k i o -> i k o")).then_inc(small_in, 16)
                sp.dma_start(r_sage[lane(h), :], sage_w[D:, :]).then_inc(small_in, 16)
            sp.dma_start(r_sage_aux[:, :, :], sage_w.rearrange("(k i) o -> i k o", k=2)).then_inc(small_in, 16)
            for k in range(NB):
                load_a(0, k, True)
                if k % 2 == 0 and k // 2 + 1 < NC:
                    load_x(NC - 2 - k // 2)
            with sp.Fori(0, NB - 1) as j:
                for k in range(NB):
                    load_a(j + 1, k, False, j)

            for s in range(NB):
                sp.wait_ge(b_out[s], 16 * NB)
            ring_loads = {s: 0 for s in range(SLOTS)}
            for n in range(6):
                for i in half_rows(n):
                    for j in half_cols(n, i):
                        k = ring_no[n, i, j]
                        s = RING[k % len(RING)]
                        if k < 4:
                            sp.wait_ge(t_ready, 4 * NB * NB)
                            sp.wait_ge(a_summed, NB * NB)
                        elif k < len(RING):
                            sp.wait_ge(av_step, NC * (NB - 1) + (k - 4) // 2 + 1)
                        else:
                            sp.wait_ge(blk_used, k - len(RING) + 1)
                        sp.dma_start(flat(s), turned[j, i]).then_inc(blk_in[s], 16)
                    if n % 2:
                        k = diag_no[n, i]
                        if k >= 2:
                            m, r = diag_list[k - 2]
                            sp.wait_ge(acc_done if m == 5 else defer_done, l_count(m, r))
                        sp.dma_start(flat(DIAG[k % 2]), turned[i, i]).then_inc(blk_in[DIAG[k % 2]], 16)
                    if n == 5 and i:
                        store_out(sp, i - 1)
            store_out(sp, NB - 1)
            sp.wait_ge(out_done, 16 * NB)

        @block_ctx.gpsimd
        def _(pool_eng):
            steps = [0]

            def step(ins):
                steps[0] += 1
                ins.then_inc(consts_step, 1)
                pool_eng.wait_ge(consts_step, steps[0])

            nc.gpsimd.memset(part[:, 0, :], 0.0).then_inc(zeros, 1)
            step(nc.gpsimd.memset(ident[:, :], 0.0))
            step(nc.gpsimd.affine_select(out=ident[:, :], in_=ident[:, :], compare_op=ALU.not_equal, fill=1.0,
                                         base=0, pattern=[[-1, P]], channel_multiplier=1))
            nc.gpsimd.tensor_tensor(fold[:, :], ident[:, 0:D], ident[:, D:P], ALU.add).then_inc(consts, 1)
            pool_eng.wait_ge(consts, 1)
            pool_eng.wait_ge(small_in, 16 * 15)
            step(nc.gpsimd.tensor_tensor(r_end[lane(0), D:], wc[lane(0), 2, :], wc[lane(0), 2, :], ALU.add))
            step(nc.gpsimd.tensor_tensor(r_end[lane(1), D:], wc[lane(1), 1, :], wc[lane(1), 3, :], ALU.subtract))
            step(nc.gpsimd.tensor_tensor(r_w3[lane(1), :], wc[lane(1), 3, :], wc[lane(1), 3, :], ALU.add))
            step(nc.gpsimd.tensor_tensor(r_aux[:, :], wc[lane(0), 0, :], wc[lane(0), 2, :], ALU.subtract))
            step(nc.gpsimd.memset(minus_half[:, :], -0.5))
            nc.gpsimd.tensor_copy(r_end[:, 0:D], fold[:, :]).then_inc(consts, 1)

            for k in range(3 * NC + 3 * NB):
                m2 = st2[:, 0:CH if k < 3 * NC else Q]
                pool_eng.wait_ge(root_asked, k + 1)
                nc.gpsimd.tensor_tensor(m2, m2, minus_half[:, 0:m2.shape[1]], ALU.pow).then_inc(root_done, 1)

        @block_ctx.tensor
        def _(pe):
            mm = nc.tensor.matmul

            def turn_h0(s):
                m = NC - 1 - s
                pe.wait_ge(h0_ready, s + 1)
                for k in range(CH):
                    ins = nc.tensor.transpose(ps[0:D, k // Q, (k % Q) * P:(k % Q + 1) * P],
                                              S[:, CH * m + k, D:], ident[:, :])
                ins.then_inc(h0_turned, 1)
                pe.wait_ge(h0_copied, s + 1)
                if s:
                    pe.wait_ge(e_ready, s)
                for k in range(CH):
                    ins = mm(ps[:, 2, D * k:D * k + D], hT[:, k // Q, (k % Q) * P:(k % Q + 1) * P],
                             w_ui[:, int(m >= NU // (CH * P)), :], start=True, stop=True)
                ins.then_inc(h0_w, 1)

            def add_v(J, k):
                pe.wait_ge(a_in[k % A_SLOTS], 16 * (2 * J + k // A_SLOTS + 1))
                for q in range(Q):
                    ins = mm(ps[lane(q % 2), V_BANK, :], S[:, Q * ORDER[k] + q, 0:D], pool[:, NB + k % A_SLOTS, q, :],
                             start=(k == 0 and q < 2), stop=(k == NB - 1 and q >= 2), skip_group_check=True)
                if k == NB - 1:
                    ins.then_inc(v_done, 1)

            def turn_tiles(J, k, g, first):
                for qj in (2 * g, 2 * g + 1):
                    c = Q * k + qj
                    if c >= 2 or not first:
                        pe.wait_ge((even_copied, odd_copied)[c % 2], 2 * NB * J + c // 2)
                    for qi in range(Q):
                        ins = nc.tensor.transpose(ps[:, T_BANKS[c % 2], qi * P:(qi + 1) * P],
                                                  pool[:, NB + k % A_SLOTS, qi, qj * P:(qj + 1) * P], ident[:, :])
                    ins.then_inc(t_ready, 1)

            def turn_v(J):
                pe.wait_ge(even_copied, 2 * NB * J + 2 * NB - 1)
                pe.wait_ge(vt_copied, J + 1)
                for q in range(Q):
                    ins = mm(ps[:, T_BANKS[0], D * q:D * q + D], vT[:, 0, q * P:(q + 1) * P], fold[:, :],
                             start=True, stop=True)
                ins.then_inc(v_turned, 1)
                pe.wait_ge(v_ready, J + 1)

            def add_av(m, q0, q1):
                for q in range(q0, q1):
                    for n in (2 * m, 2 * m + 1):
                        ins = mm(ps[lane(n % 2), m, :], v_rows[:, q, :], pool[:, n, q, :],
                                 start=False, stop=False, skip_group_check=True)
                if q1 == Q:
                    ins.then_inc(av_step, 1)

            def panel(J, first):
                for s in range(NC):
                    m = NC - 1 - s
                    if first:
                        turn_h0(s)
                        pe.wait_ge(e_ready, s + 1)
                    k = 2 * s
                    add_v(J, k)
                    turn_tiles(J, k, 0, first)
                    add_v(J, k + 1)
                    turn_tiles(J, k, 1, first)
                    if s < NC - 1:
                        if not first:
                            add_av(m - 1, 0, Q // 2)
                        turn_tiles(J, k + 1, 0, first)
                        if not first:
                            add_av(m - 1, Q // 2, Q)
                        turn_tiles(J, k + 1, 1, first)
                    else:
                        turn_tiles(J, k + 1, 0, first)
                        if first:
                            pe.wait_ge(zeros, 1)
                            for c in range(NC):
                                for h in range(2):
                                    mm(ps[lane(h), c, :], part[:, 0, 0:D], part[:, 0, :], start=True, stop=False,
                                       skip_group_check=True)
                        turn_v(J)
                        turn_tiles(J, k + 1, 1, first)
                        add_av(NC - 1, 0, Q)

            pe.wait_ge(consts, 1)
            pe.wait_ge(small_in, 16 * 15)
            nc.tensor.transpose(ps[:, 3, 0:NT], diag_rows[:, :], ident[0:NT, 0:NT]).then_inc(diag_turned, 1)
            panel(0, True)
            with pe.Fori(1, NB) as J:
                panel(J, False)
            pe.wait_ge(even_copied, 2 * NB * NB)
            pe.wait_ge(odd_copied, 2 * NB * NB)

            def turn_av(k):
                pe.wait_ge(gt_copied, k + 1)
                if k >= 2:
                    pe.wait_ge(g_ready, k - 1)
                for q in range(Q):
                    ins = nc.tensor.transpose(ps[:, T_BANKS[k % 2], q * P:(q + 1) * P],
                                              yT[:, k % 2, q * P:(q + 1) * P], ident[:, :])
                ins.then_inc(g_turned, 1)

            for k in range(NC):
                if k:
                    add_av(NC - 1 - k, 0, Q)
                    turn_av(k - 1)
            turn_av(NC - 1)

            def wait_block(n, i, j):
                k = ring_no[n, i, j]
                pe.wait_ge(blk_in[RING[k % len(RING)]], 16 * (k // len(RING) + 1))
                return pool[:, RING[k % len(RING)], :, :]

            def wait_diag(n, i):
                k = diag_no[n, i]
                pe.wait_ge(blk_in[DIAG[k % 2]], 16 * (k // 2 + 1))
                return pool[:, DIAG[k % 2], :, :]

            def wait_bank(n, i):
                k = panel_number(n, i)
                if k < 3:
                    pe.wait_ge(gt_copied, k + 1)
                if k >= 4:
                    m, r = [(a, b) for a in range(6) for b in half_rows(a)][k - 4]
                    if m:
                        pe.wait_ge(y_ready, ended(m, r))
                    if m == 5:
                        pe.wait_ge(y_upper, NB - 1 + r + 1)
                    elif m % 2 and r == NB - 1:
                        pe.wait_ge(y_ready, ended(m + 1, r))
                    else:
                        pe.wait_ge(part_saved, saved(m + 1, r))
                return ACC_BANKS[k % 4]

            def off_diagonal(n, i, j, bank, start, stop):
                b = wait_block(n, i, j)
                if n == 0:
                    pe.wait_ge(h1_ready, h1_chunk(j))
                else:
                    pe.wait_ge(op_ready, ended(min(n, 4), j))
                for q in range(Q):
                    if n in (0, 5):
                        ins = mm(ps[lane(q % 2), bank, :], S[:, Q * j + q, 0:D], b[:, q, :],
                                 start=start and q < 2, stop=stop and q >= 2, skip_group_check=True)
                    else:
                        ins = mm(ps[:, bank, :], S[:, Q * j + q, :], b[:, q, :],
                                 start=start and q == 0, stop=stop and q == Q - 1, skip_group_check=True)
                return ins

            def on_diagonal(n, i):
                own = lane(n % 2 == 0)
                other = lane(n % 2)
                ins = dins = None
                if i < NB:
                    b = wait_diag(n, i)
                    pe.wait_ge(op_ready, ended(n - 1, i)) if n > 1 else pe.wait_ge(h1_ready, h1_chunk(i))
                    bank = ACC_BANKS[panel_number(n, i) % 4]
                if n < 5 and i > 0:
                    d = wait_diag(n, i - 1)
                    pe.wait_ge(op_ready, ended(n, i - 1))
                    dbank = ACC_BANKS[panel_number(n, i - 1) % 4]
                for q in range(Q):
                    if i < NB and n == 5:
                        ins = mm(ps[lane(q % 2), bank, :], S[:, Q * i + q, own], b[:, q, :],
                                 start=(i == 0 and q < 2), stop=(q >= 2), skip_group_check=True)
                    elif i < NB:
                        ins = mm(ps[own, bank, :], S[:, Q * i + q, own], b[:, q, :],
                                 start=(i == 0 and q == 0), stop=(q == Q - 1), skip_group_check=True)
                    if q == Q - 1 and ins is not None:
                        ins.then_inc(acc_done, 1)
                    if n < 5 and i > 0:
                        dins = mm(ps[other, dbank, :], S[:, Q * (i - 1) + q, other], d[:, q, :],
                                  start=(i == 1 and q == 0), stop=(q == Q - 1), skip_group_check=True)
                if dins is not None:
                    dins.then_inc(defer_done, 1)

            def end_rows(n, i):
                c = ended(n, i)
                pe.wait_ge(y_ready, c)
                if n == 1 and i < NB - 1:
                    pe.wait_ge(y_upper, i + 1)
                if n == 5:
                    pe.wait_ge(y_upper, NB - 1 + i + 1)
                if c > 2:
                    pe.wait_ge(rows_read, c - 2)
                sl, rhs = {
                    1: (slice(0, P) if i < NB - 1 else lane(0), fold[:, :]),
                    2: (lane(1), r_end[:, :]),
                    3: (lane(0), r_end[:, :]),
                    4: (lane(1), r_w3[:, :]),
                    5: (slice(0, P), r_sage[:, :]),
                }[n]
                w = rhs.shape[1]
                for q in range(Q):
                    ins = mm(ps[:, T_BANKS[c % 2], P * q:P * q + w], yT[sl, c % 2, q * P:(q + 1) * P], rhs[sl, :],
                             start=True, stop=True)
                ins.then_inc(rows_ready, 1)

            def aux_turn(u):
                i = u % NB
                if u:
                    pe.wait_ge(ht_copied, u)
                pe.wait_ge(op_ready, ended(1, i) if u < NB else ended(4, i))
                src = lane(u < NB)
                for q in range(Q):
                    ins = nc.tensor.transpose(ps[0:D, HT_BANK, q * P:(q + 1) * P], S[:, Q * i + q, src], ident[:, :])
                ins.then_inc(ht_done, 1)

            def aux_mul(u):
                pe.wait_ge(ht_copied, u + 1)
                if u:
                    pe.wait_ge(aux_read, u)
                rhs = r_aux[:, :] if u < NB else r_sage_aux[:, :, :].rearrange("p k d -> p (k d)")
                w = rhs.shape[1]
                for q in range(Q):
                    ins = mm(ps[:, AUX_BANK, P * q:P * q + w], hT[:, u % 2, q * P:(q + 1) * P], rhs,
                             start=True, stop=True)
                ins.then_inc(aux_done, 1)

            pe.wait_ge(consts, 2)
            for n in range(6):
                pending = None
                if n in (2, 4):
                    end_rows(n, NB - 1)

                def flush(i, n=n):
                    end_rows(n, i)
                    if n == 1:
                        if i >= 2:
                            aux_mul(i - 2)
                        if i >= 1:
                            aux_turn(i - 1)

                for i in half_rows(n):
                    bank = wait_bank(n, i)
                    cols = half_cols(n, i)
                    for idx, j in enumerate(cols):
                        if n and pending is not None and j == pending:
                            flush(pending)
                            pending = None
                        ins = off_diagonal(n, i, j, bank, idx == 0, n % 2 == 0 and idx == len(cols) - 1)
                        ins.then_inc(blk_used, 1)
                        if n and pending is not None and idx == 0:
                            flush(pending)
                            pending = None
                        if n == 5 and idx == 0:
                            aux_turn(NB + i)
                    if n % 2:
                        if n == 5 and i == 0:
                            aux_turn(NB)
                        on_diagonal(n, i)
                    if n == 5:
                        aux_mul(NB + i)
                    pending = i
                if n:
                    flush(pending)
                if n == 1:
                    aux_mul(NB - 2)
                if n in (1, 3):
                    on_diagonal(n, NB)
                if n == 1:
                    aux_turn(NB - 1)
                    aux_mul(NB - 1)

        @block_ctx.scalar
        def _(act):
            def panel(J, first):
                for k in range(NB):
                    s, n = k // 2, ORDER[k]
                    if first and k % 2 == 0:
                        act.wait_ge(h0_turned, s + 1)
                        if s:
                            act.wait_ge(h0_w, s)
                        nc.scalar.copy(hT[:, :, :], ps[0:D, 0:2, :]).then_inc(h0_copied, 1)
                    if not first:
                        act.wait_ge(av_step, NC * J - (NC - 1 - s))
                        act.wait_ge(b_out[n], 16 * J)
                    for qj in range(Q):
                        c = Q * k + qj
                        if qj % 2 or first:
                            act.wait_ge(t_ready, Q * NB * J + c + 1)
                            nc.scalar.copy(pool[:, n, qj, :], ps[:, T_BANKS[qj % 2], :]).then_inc(
                                (even_copied, odd_copied)[qj % 2], 1)
                        if c == Q * NB - 7:
                            act.wait_ge(v_done, J + 1)
                            nc.scalar.copy(vT[:, 0, :], ps[:, V_BANK, :]).then_inc(vt_copied, 1)
                    act.wait_ge(even_copied, 2 * NB * J + 2 * k + 2)
                    act.wait_ge(odd_copied, 2 * NB * J + 2 * k + 2)
                    act.dma_start(turned_panel(J, n), flat(n)).then_inc(b_out[n], 16)

            panel(0, True)
            with act.Fori(1, NB) as J:
                panel(J, False)

            def copy_gt(k):
                act.wait_ge(av_step, NC * (NB - 1) + k + 1)
                if k >= 2:
                    act.wait_ge(g_turned, k - 1)
                nc.scalar.copy(yT[:, k % 2, :], ps[:, NC - 1 - k, :]).then_inc(gt_copied, 1)

            def copy_g(k):
                act.wait_ge(g_turned, k + 1)
                if k >= 2:
                    act.wait_ge(h1_ready, k - 1)
                nc.scalar.copy(g[:, k % 2, :, :].rearrange("p (b q) d -> p b q d", b=2),
                               ps[:, T_BANKS[k % 2], :].rearrange("p (q b d) -> p b q d", q=Q, b=2)).then_inc(g_ready, 1)

            for k in range(NC):
                copy_gt(k)
                if k:
                    copy_g(k - 1)
            copy_g(NC - 1)

            def save(n, i):
                m = n - 1
                if m % 2:
                    act.wait_ge(defer_done, l_count(m, i))
                else:
                    act.wait_ge(blk_used, ring_no[m, i, i + 1] + 1)
                if n == 2:
                    act.wait_ge(y_upper, i + 1)
                sl = slice(0, P) if n == 1 else lane(n % 2 == 0)
                nc.scalar.copy(part[sl, i, :], ps[sl, ACC_BANKS[panel_number(m, i) % 4], :]).then_inc(part_saved, 1)

            def upper(n, i):
                c = ended(n, i)
                if c > 2:
                    act.wait_ge(rows_ready, c - 2)
                if n == 1:
                    act.wait_ge(part_saved, saved(1, i))
                    src = part[lane(1), i, :]
                else:
                    act.wait_ge(acc_done, l_count(5, i))
                    src = ps[lane(1), ACC_BANKS[panel_number(5, i) % 4], :]
                nc.scalar.copy(yT[lane(1), c % 2, :], src).then_inc(y_upper, 1)

            def copy_ht(u):
                act.wait_ge(ht_done, u + 1)
                if u >= 2:
                    act.wait_ge(aux_done, u - 1)
                nc.scalar.copy(hT[:, u % 2, :], ps[0:D, HT_BANK, :]).then_inc(ht_copied, 1)

            for i in half_rows(0):
                save(1, i)
            for i in range(NB + 1):
                if 1 <= i < NB:
                    upper(1, i - 1)
                if i >= 2:
                    copy_ht(i - 2)
                if 1 <= i < NB:
                    save(2, i - 1)
            copy_ht(NB - 1)
            for i in half_rows(2):
                save(3, i)
            for i in range(NB - 1):
                save(4, i)
            for i in half_rows(4):
                save(5, i)
            for i in range(NB):
                if i:
                    upper(5, i - 1)
                copy_ht(NB + i)
                act.wait_ge(aux_done, NB + i + 1)
                if i >= 2:
                    act.wait_ge(fin_step, i - 1)
                nc.scalar.copy(g[:, i % 2, :, :].rearrange("p t d -> p (t d)"), ps[:, AUX_BANK, :]).then_inc(aux_read, 1)
            upper(5, NB - 1)

        @block_ctx.vector
        def _(dve):
            vec = nc.vector
            steps = [0]

            def step(ins):
                steps[0] += 1
                ins.then_inc(dve_step, 1)
                dve.wait_ge(dve_step, steps[0])

            roots = [0]

            def wait_root():
                roots[0] += 1
                dve.wait_ge(root_done, roots[0])

            def cols(stat, t):
                return stat.unsqueeze(2).to_broadcast([P, t, D])

            def rows(vecs, t):
                return vecs.unsqueeze(1).to_broadcast([P, t, D])

            def normalise(src, t):
                a, b, m1, m2 = tmp[:, 0:t, :], tmp2[:, 0:t, :], st1[:, 0:t], st2[:, 0:t]
                step(vec.tensor_reduce(m1, src, AX.X, ALU.add))
                step(vec.scalar_tensor_tensor(out=a, in0=cols(m1, t), scalar=-1.0 / D, in1=src, op0=ALU.mult, op1=ALU.add))
                step(vec.tensor_tensor(b, a, a, ALU.mult))
                step(vec.tensor_reduce(m2, b, AX.X, ALU.add))
                vec.tensor_scalar(m2, m2, D * EPS, None, ALU.add).then_inc(root_asked, 1)
                wait_root()
                step(vec.tensor_tensor(a, a, cols(m2, t), ALU.mult))
                return a

            def relu_norm(src, dst, t):
                return vec.tensor_scalar(dst, normalise(src, t), 8.0, 0.0, ALU.mult, ALU.max)

            def make_e(s):
                m = NC - 1 - s
                c = slice(CH * m, CH * m + CH)
                dve.wait_ge(x_in[m], 16)
                relu_norm(X[:, c, :], S[:, c, D:], CH).then_inc(h0_ready, 1)
                dve.wait_ge(h0_ready, s + 1)
                step(vec.tensor_tensor(X[:, c, :], X[:, c, :], S[:, c, D:], ALU.add))
                if s == 0:
                    dve.wait_ge(small_in, 16 * 15)
                    step(vec.tensor_tensor(cpar[:, :], pars[:, 0:4:2], pars[:, 1:4:2], ALU.mult))
                    dve.wait_ge(diag_turned, 1)
                    nu = NU // P
                    step(vec.tensor_scalar(cdiag[:, 0:nu], ps[:, 3, 0:nu], cpar[:, 0:1], None, ALU.mult))
                    step(vec.tensor_scalar(cdiag[:, nu:], ps[:, 3, nu:NT], cpar[:, 1:2], None, ALU.mult))
                    step(vec.tensor_scalar(gamma8[:, :], gamma8[:, :], 8.0, None, ALU.mult))
                step(vec.tensor_tensor(X[:, c, :], X[:, c, :], rows(beta[:, :], CH), ALU.add))
                dve.wait_ge(h0_w, s + 1)
                step(vec.tensor_tensor(tmp[:, :, :], ps[:, 2, :].rearrange("p (t d) -> p t d", t=CH),
                                       cols(cdiag[:, c], CH), ALU.mult))
                vec.tensor_tensor(S[:, c, 0:D], tmp[:, :, :], S[:, c, D:], ALU.add).then_inc(e_ready, 1)
                dve.wait_ge(e_ready, s + 1)

            def panel(J, first):
                if first:
                    make_e(0)
                for k in range(NB):
                    s, n = k // 2, ORDER[k]
                    if not first:
                        dve.wait_ge(av_step, NC * J - (NC - 1 - s))
                        dve.wait_ge(b_out[n], 16 * J)
                    for h in range(2):
                        c = Q * k + 2 * h
                        if c == Q * NB - 2:
                            copy_v(J)
                        if not first:
                            dve.wait_ge(t_ready, Q * NB * J + c + 1)
                            vec.tensor_copy(pool[:, n, 2 * h, :], ps[:, T_BANKS[0], :]).then_inc(even_copied, 1)
                        if h == 0:
                            dve.wait_ge(a_in[k % A_SLOTS], 16 * (2 * J + k // A_SLOTS + 1))
                            if not first:
                                dve.wait_ge(rs_added, NB * J - (NB - 1 - k))
                        ins = vec.tensor_reduce(rs_part[:, n, 2 * h:2 * h + 2],
                                                pool[:, NB + k % A_SLOTS, 2 * h:2 * h + 2, :], AX.X, ALU.add)
                    ins.then_inc(a_summed, 1)
                    dve.wait_ge(a_summed, NB * J + k + 1)
                    r = rowsum[:, Q * n:Q * n + Q]
                    vec.tensor_tensor(r, r, rs_part[:, n, :], ALU.add).then_inc(rs_added, 1)
                    if first and k % 2 and s < NC - 1:
                        make_e(s + 1)

            def copy_v(J):
                dve.wait_ge(v_turned, J + 1)
                vec.tensor_copy(v_rows[:, :, :].rearrange("p q d -> p (q d)"), ps[:, T_BANKS[0], 0:Q * D]).then_inc(v_ready, 1)

            step(vec.memset(rowsum[:, :], 0.0))
            panel(0, True)
            with dve.Fori(1, NB) as J:
                panel(J, False)

            dve.wait_ge(rs_added, NB * NB)
            step(vec.tensor_scalar(rdeg[:, :], rowsum[:, :], 1.0, 1.0, ALU.add, ALU.max))
            step(vec.reciprocal(rdeg[:, :], rdeg[:, :]))

            for k in range(NC):
                c = slice(CH * (NC - 1 - k), CH * (NC - k))
                dve.wait_ge(g_ready, k + 1)
                a = normalise(g[:, k % 2, :, :], CH)
                step(vec.tensor_tensor(a, a, rows(gamma8[:, :], CH), ALU.mult))
                step(vec.tensor_tensor(X[:, c, :], X[:, c, :], a, ALU.add))
                relu_norm(X[:, c, :], S[:, c, 0:D], CH).then_inc(h1_ready, 1)
                dve.wait_ge(h1_ready, k + 1)

            def end_sum(n, i):
                c = ended(n, i)
                h = lane(n % 2 == 0)
                m = n if n % 2 or i < NB - 1 else n - 1
                if m % 2 == 0:
                    dve.wait_ge(blk_used, ring_no[n, i, i + 1] + 1)
                elif m == n:
                    dve.wait_ge(acc_done, l_count(n, i))
                else:
                    dve.wait_ge(defer_done, l_count(m, i))
                if c > 2:
                    dve.wait_ge(rows_ready, c - 2)
                acc = ps[h, ACC_BANKS[panel_number(m, i) % 4], :]
                if i < NB - 1:
                    dve.wait_ge(part_saved, saved(n, i))
                    vec.tensor_tensor(yT[h, c % 2, :], acc, part[h, i, :], ALU.add).then_inc(y_ready, 1)
                else:
                    vec.tensor_copy(yT[h, c % 2, :], acc).then_inc(y_ready, 1)

            def end_layer(n, i):
                c = ended(n, i)
                ti = slice(Q * i, Q * i + Q)
                x_i, odd, even = X[:, ti, :], S[:, ti, 0:D], S[:, ti, D:]
                r = ps[:, T_BANKS[c % 2], :].rearrange("p (q k d) -> p q k d", q=Q, k=2)
                r0, r1 = r[:, :, 0, :], r[:, :, 1, :]
                a, b, m1 = tmp[:, 0:Q, :], tmp2[:, 0:Q, :], st1[:, 0:Q]
                dve.wait_ge(rows_ready, c)

                def read(ins):
                    ins.then_inc(rows_read, 1)
                    dve.wait_ge(rows_read, c)

                if n == 1:
                    read(vec.tensor_tensor(a, r0, odd, ALU.mult))
                    step(vec.tensor_reduce(m1, a, AX.X, ALU.add))
                    step(vec.tensor_scalar(m1, m1, -0.01, 1.0, ALU.mult, ALU.add))
                    step(vec.scalar_tensor_tensor(out=a, in0=odd, scalar=-0.1, in1=x_i, op0=ALU.mult, op1=ALU.add))
                    step(vec.tensor_tensor(x_i, a, cols(m1, Q), ALU.add))
                    relu_norm(x_i, even, Q).then_inc(op_ready, 1)
                elif n == 2:
                    vec.tensor_copy(odd, r0).then_inc(op_ready, 1)
                    read(vec.tensor_tensor(x_i, x_i, r1, ALU.add))
                elif n == 3:
                    vec.scalar_tensor_tensor(out=even, in0=r0, scalar=2.0, in1=even, op0=ALU.mult,
                                             op1=ALU.subtract).then_inc(op_ready, 1)
                    read(vec.tensor_tensor(x_i, x_i, r1, ALU.add))
                elif n == 4:
                    read(vec.tensor_tensor(x_i, x_i, r0, ALU.add))
                    relu_norm(x_i, odd, Q).then_inc(op_ready, 1)
                else:
                    dve.wait_ge(aux_read, NB + i + 1)
                    gi = g[:, i % 2, :, :].rearrange("p (q k) d -> p q k d", k=2)
                    read(vec.tensor_tensor(a, r0, gi[:, :, 1, :], ALU.add))
                    step(vec.tensor_tensor(a, a, cols(rdeg[:, ti], Q), ALU.mult))
                    step(vec.tensor_tensor(a, a, gi[:, :, 0, :], ALU.add))
                    step(vec.tensor_tensor(a, a, rows(b_sage[:, :], Q), ALU.add))
                    step(vec.tensor_scalar(a, a, 0.0, None, ALU.max))
                    step(vec.tensor_tensor(b, a, a, ALU.mult))
                    step(vec.tensor_reduce(m1, b, AX.X, ALU.add))
                    vec.tensor_scalar(st2[:, 0:Q], m1, 1e-24, None, ALU.max).then_inc(root_asked, 1)
                    wait_root()
                    step(vec.tensor_tensor(a, a, cols(st2[:, 0:Q], Q), ALU.mult))
                    vec.tensor_tensor(x_i, x_i, a, ALU.add).then_inc(fin_step, 1)
                    dve.wait_ge(fin_step, i + 1)
                if n < 5:
                    dve.wait_ge(op_ready, c)

            def add_aux(i):
                x_i = X[:, Q * i:Q * i + Q, :]
                dve.wait_ge(aux_done, i + 1)
                ps_i = ps[:, AUX_BANK, :].rearrange("p (q k) -> p q k", q=Q)[:, :, 0:D]
                vec.tensor_tensor(x_i, x_i, ps_i, ALU.add).then_inc(aux_read, 1)
                dve.wait_ge(aux_read, i + 1)
                step(vec.tensor_tensor(x_i, x_i, rows(b_cheb[:, :], Q), ALU.add))

            for n in range(1, 6):
                if n % 2 == 0:
                    end_sum(n, NB - 1)
                    if n == 2:
                        add_aux(NB - 2)
                        add_aux(NB - 1)
                    end_layer(n, NB - 1)
                for i in half_rows(n):
                    end_sum(n, i)
                    end_layer(n, i)
                    if n == 1 and i >= 2:
                        add_aux(i - 2)


_INS = ["x", "adj", "L0_gnn_W_u", "L0_gnn_diag_u", "L0_gnn_par_u", "L0_gnn_W_i", "L0_gnn_diag_i", "L0_gnn_par_i",
        "L0_gnn_ln_gamma", "L0_gnn_ln_beta", "L1_gnn_t", "L2_gnn_weight", "L2_gnn_bias", "L3_gnn_W", "L3_gnn_b"]


def kernel(**inputs):
    import numpy as _np
    import concourse.bacc as _bacc
    from concourse import mybir as _mybir
    from concourse.bass_utils import run_bass_kernel_spmd as _run

    nc = _bacc.Bacc("TRN2", target_bir_lowering=False, num_devices=1)
    arrays, args = {}, []
    for name in _INS:
        a = _np.ascontiguousarray(inputs[name])
        arrays[f"in_{name}"] = a
        args.append(nc.dram_tensor(f"in_{name}", a.shape, _mybir.dt.from_np(a.dtype), kind="ExternalInput").ap())
    args.append(nc.dram_tensor("out", (N, D), F32, kind="ExternalOutput").ap())
    graph_layers(nc, *args)
    r = _run(nc, [arrays], core_ids=[0])
    return r.results[0]["out"]
```

```python
from contextlib import ExitStack

import concourse.bass as bass
from concourse import mybir

P = 128
D = 64
BW = 512
Q = BW // P
N = 5120
NB = N // BW
NT = N // P
CH = 2 * Q
NC = NT // CH
NU = 2048
EPS = 1e-5
A_SLOTS = 5
SLOTS = A_SLOTS + NB
ORDER = [8, 9, 6, 7, 4, 5, 2, 3, 0, 1]
T_BANKS = (6, 7)
V_BANK = 5
ACC_BANKS = (5, 4, 3)
P1_BANK = 2
HT_BANK, AUX_BANK = 1, 0
P1_LATE = (3, 4)
P1_ORDER = [i for i in range(NB) if i not in P1_LATE] + list(P1_LATE)
ODD, EVEN, H1 = range(3)

H_UNITS = [slice(NT - Q, NT), slice(NT - CH, NT - Q)] + [slice(CH * m, CH * m + CH) for m in range(NC - 2, -1, -1)]

ALU = mybir.AluOpType
F32 = mybir.dt.float32
AX = mybir.AxisListType


def half_rows(m):
    return list(range(NB)) if m % 2 else [0] + list(range(NB - 2, 0, -1)) if m == 4 else list(range(NB - 2, -1, -1))


def half_cols(m, i):
    return list(range(i)) if m % 2 else list(range(1, NB)) if (m, i) == (4, 0) else list(range(NB - 1, i, -1))


def first_blocks():
    def stage(block):
        i, j = block
        if i >= NB - 6:
            return 0 if j == NB - 1 and i >= NB - 5 else 1 if j >= NB - 2 else 2 if j >= NB - 4 else 4
        return 3 if i == NB - 7 and j >= NB - 4 else 4
    return sorted([(i, j) for i in half_rows(0) for j in half_cols(0, i)], key=stage)


def end_order(n):
    if n % 2 == 0:
        return list(range(NB))
    return [0] + list(range(NB - 1, 0, -1)) if n == 5 else list(range(NB - 1, -1, -1))


PANELS = [(m, i) for m in range(5) for i in half_rows(m)]


def ended(n, i):
    return NB * (n - 2) + end_order(n).index(i) + 1


def saved(m, i):
    return (NB - 1) * m + (i if m % 2 else NB - 2 - i) + 1


def p1_half(i):
    return 3 if i in P1_LATE else 1


def aux_number(kind, i):
    return i if kind == "h2" else NB + P1_LATE.index(i) if kind == "P1" else NB + len(P1_LATE) + i


def p1_aux(i):
    return aux_number("P1" if i in P1_LATE else "h2", i)


def late_p1(at):
    blocks = [(i, j) for i in P1_LATE for j in range(i + 1)]
    return blocks[(0, 3, 7)[at]:(3, 7, 9)[at]]


def l_count(m, i):
    return NB * (m // 2) + i + 1


def plan_blocks():
    use, release, told = [], {}, {}
    for i, j in first_blocks():
        use.append((0, i, j))
        release[0, i, j], told[0, i, j] = len(use), ("blk_used", len(use))
    n_off = len(use)
    for m, i in PANELS[NB - 1:]:
        cols = half_cols(m, i)
        if m % 2:
            cols.insert(len(cols) - 1 if m == 1 and cols and i not in P1_LATE else len(cols), i)
        for at, j in enumerate(cols):
            if m == 3 and i < 3 and at == 0:
                use += [(3, *b) for b in late_p1(i)]
            if (m, i, j) not in use:
                use.append((m, i, j))
            if j != i:
                n_off += 1
                release[m, i, j], told[m, i, j] = len(use), ("blk_used", n_off)
        if m % 2 and i:
            release[m, i - 1, i - 1], told[m, i - 1, i - 1] = len(use), ("defer_done", l_count(m, i - 1))
        if (m, i) == (1, NB - 1):
            release[1, i, i], told[1, i, i] = len(use), ("defer_done", l_count(1, i))
        if (m, i) == (4, 0):
            release[3, NB - 1, NB - 1], told[3, NB - 1, NB - 1] = len(use), ("defer_done", l_count(3, NB - 1))
    holds = {s: (0, s, NB - 1) for s in range(NB - 1)}
    free_at = {s: release[holds[s]] for s in holds}
    wait = {s: told[holds[s]] for s in holds}
    free_at[NB - 1], wait[NB - 1] = -1, ("av_step", NC * (NB - 1) + 1)
    for s in range(NB, NB + A_SLOTS):
        free_at[s], wait[s] = -2, ("gathered", 0)
    plan = {b: (s, 0, None) for s, b in holds.items()}
    loads = {s: 0 for s in range(SLOTS)}
    for at, b in enumerate(use):
        if b in plan:
            continue
        s = min(free_at, key=lambda k: free_at[k])
        assert free_at[s] <= at
        loads[s] += 1
        plan[b] = (s, loads[s], wait[s])
        free_at[s], wait[s] = release[b], told[b]
    return use, plan, {b: t[1] for b, t in told.items() if t[0] == "blk_used"}


def graph_layers(nc, x, adj, W_u, diag_u, par_u, W_i, diag_i, par_i, ln_gamma, ln_beta, t, cheb_w, cheb_b,
                 sage_w, sage_b, out):
    with ExitStack() as ctx:
        def sb(name, shape):
            return ctx.enter_context(nc.sbuf_tensor(name, shape, F32))

        def sem(name):
            return ctx.enter_context(nc.semaphore(name))

        turned = nc.dram_tensor("turned", [NB, NB, P, Q * BW], F32).ap()

        pool = sb("pool", [P, SLOTS, Q, BW])
        X = sb("X", [P, NT, D])
        S = sb("S", [P, NT, 3, D])
        part = sb("part", [P, NB, BW])
        yT = sb("yT", [P, 2, BW])
        y1 = sb("y1", [P, 2, BW])
        hT = sb("hT", [D, 2, BW])
        g = sb("g", [P, 2, CH, D])
        p1_kept = g[0:D, :, :, :].rearrange("p k t d -> p k (t d)")
        tmp = sb("tmp", [P, CH, D])
        tmp2 = sb("tmp2", [P, CH, D])
        st1 = sb("st1", [P, CH])
        st2 = sb("st2", [P, CH])
        vT = yT
        minus_half = sb("minus_half", [P, CH])
        v_rows = part[:, 1, 0:Q * D].rearrange("p (q d) -> p q d", q=Q)
        w_ui = part[0:D, 2, 0:2 * D].rearrange("p (k d) -> p k d", k=2)
        diag_rows = part[0:NT, 3, 0:P]
        wc = part[:, 4, 0:4 * D].rearrange("p (k d) -> p k d", k=4)
        rowsum = sb("rowsum", [P, NT])
        rs_part = sb("rs_part", [P, NB, Q])
        rdeg = sb("rdeg", [P, NT])
        ident = sb("ident", [P, P])
        fold = sb("fold", [P, D])
        pars = sb("pars", [P, 4])
        cpar = sb("cpar", [P, 2])
        cdiag = sb("cdiag", [P, NT])
        gamma8 = sb("gamma8", [P, D])
        beta = sb("beta", [P, D])
        b_cheb = sb("b_cheb", [P, D])
        b_sage = sb("b_sage", [P, D])
        r_end = sb("r_end", [P, 2 * D])
        r_w3 = sb("r_w3", [P, D])
        r_aux = sb("r_aux", [D, D])
        r_sage = sb("r_sage", [P, D])
        r_sage_aux = sb("r_sage_aux", [D, 2, D])
        ps = ctx.enter_context(nc.psum_tensor("ps", [P, 8, BW], F32))

        x_in = [sem(f"x_in{m}") for m in range(NC)]
        gather_in = sem("gather_in")
        small_in = sem("small_in")
        consts_step = sem("consts_step")
        consts = sem("consts")
        zeros = sem("zeros")
        a_in = [sem(f"a_in{s}") for s in range(A_SLOTS)]
        b_out = [sem(f"b_out{s}") for s in range(NB)]
        diag_turned = sem("diag_turned")
        h0_asked = sem("h0_asked")
        h0_ready = sem("h0_ready")
        h0_turned = sem("h0_turned")
        h0_copied = sem("h0_copied")
        h0_w = sem("h0_w")
        e_ready = sem("e_ready")
        residual = sem("residual")
        acc_zero = sem("acc_zero")
        t_ready = sem("t_ready")
        even_copied = sem("even_copied")
        odd_copied = sem("odd_copied")
        a_summed = sem("a_summed")
        rs_added = sem("rs_added")
        v_added = sem("v_added")
        v_done = sem("v_done")
        vt_copied = sem("vt_copied")
        v_turned = sem("v_turned")
        v_ready = sem("v_ready")
        av_step = sem("av_step")
        gt_copied = sem("gt_copied")
        g_turned = sem("g_turned")
        g_ready = sem("g_ready")
        h_ready = sem("h_ready")
        h1_kept = sem("h1_kept")
        late_kept = sem("late_kept")
        blk_in = [sem(f"blk_in{s}") for s in range(SLOTS)]
        blk_used = sem("blk_used")
        acc_done = sem("acc_done")
        defer_done = sem("defer_done")
        part_saved = sem("part_saved")
        p1_done = sem("p1_done")
        y1_ready = sem("y1_ready")
        y1_upper = sem("y1_upper")
        y_ready = sem("y_ready")
        y_upper = sem("y_upper")
        rows_ready = sem("rows_ready")
        rows_read = sem("rows_read")
        op_ready = sem("op_ready")
        ht_done = sem("ht_done")
        ht_copied = sem("ht_copied")
        aux_done = sem("aux_done")
        aux_read = sem("aux_read")
        fin_step = sem("fin_step")
        out_done = sem("out_done")
        dve_step = sem("dve_step")
        root_asked = sem("root_asked")
        root_done = sem("root_done")

        use, plan, used_no = plan_blocks()

        def block(s):
            return pool[:, s, :, :]

        def flat(s):
            return pool[:, s, :, :].rearrange("p q i -> p (q i)")

        def lane(odd):
            return slice(D, 2 * D) if odd else slice(0, D)

        def turned_panel(J, n):
            if isinstance(J, int):
                return turned[J, n]
            return turned.rearrange("a n p f -> (a n p) f")[bass.ds(J * (NB * P) + n * P, P), :]

        def h_there(j):
            return next(u for u, tiles in enumerate(H_UNITS) if tiles.start <= Q * j < tiles.stop) + 1

        block_ctx = ctx.enter_context(nc.Block())

        def store_out(sp, i):
            sp.wait_ge(fin_step, end_order(5).index(i) + 1)
            dst = out[i * BW:(i + 1) * BW, :].rearrange("(q p) d -> p q d", p=P)
            sp.dma_start(dst, X[:, Q * i:Q * i + Q, :]).then_inc(out_done, 16)

        @block_ctx.sync
        def _(sp):
            def load_a(J, k, first, j=0):
                s, n = k % A_SLOTS, ORDER[k]
                rows = adj[n * BW:(n + 1) * BW, 0 if first else BW:]
                src = rows[:, bass.ts(J if first else j, BW)].rearrange("(q p) j -> p q j", p=P)
                if not (first and k < A_SLOTS):
                    sp.wait_ge(t_ready, Q * (NB * J + k - A_SLOTS + 1))
                    sp.wait_ge(a_summed, NB * J + k - A_SLOTS + 1)
                    if first:
                        sp.wait_ge(v_added, k - A_SLOTS + 1)
                sp.dma_start(block(NB + s), src).then_inc(a_in[s], 16)

            def load_x(m):
                xr = x.rearrange("(t p) d -> p t d", p=P)
                sp.dma_start(X[:, CH * m:CH * m + CH, :], xr[:, CH * m:CH * m + CH, :]).then_inc(x_in[m], 16)

            load_x(NC - 1)
            load_a(0, 0, True)
            sp.dma_start(w_ui[:, 0, :], W_u).then_inc(gather_in, 16)
            sp.dma_start(w_ui[:, 1, :], W_i).then_inc(gather_in, 16)
            sp.dma_start(diag_rows[0:NU // P, :], diag_u.rearrange("(t p) -> t p", p=P)).then_inc(gather_in, 16)
            sp.dma_start(diag_rows[NU // P:, :], diag_i.rearrange("(t p) -> t p", p=P)).then_inc(gather_in, 16)
            sp.dma_start(pars[:, 0:2], par_u.partition_broadcast(P)).then_inc(gather_in, 16)
            sp.dma_start(pars[:, 2:4], par_i.partition_broadcast(P)).then_inc(gather_in, 16)
            load_x(NC - 2)
            for k in range(1, A_SLOTS):
                load_a(0, k, True)
                if k == 2:
                    load_x(NC - 3)
            sp.dma_start(gamma8[:, :], ln_gamma.partition_broadcast(P)).then_inc(small_in, 16)
            sp.dma_start(beta[:, :], ln_beta.partition_broadcast(P)).then_inc(small_in, 16)
            sp.dma_start(b_cheb[:, :], cheb_b.partition_broadcast(P)).then_inc(small_in, 16)
            sp.dma_start(b_sage[:, :], sage_b.partition_broadcast(P)).then_inc(small_in, 16)
            for h in range(2):
                sp.dma_start(wc[lane(h), :, :], cheb_w.rearrange("k i o -> i k o")).then_inc(small_in, 16)
                sp.dma_start(r_sage[lane(h), :], sage_w[D:, :]).then_inc(small_in, 16)
            sp.dma_start(r_sage_aux[:, :, :], sage_w.rearrange("(k i) o -> i k o", k=2)).then_inc(small_in, 16)
            load_x(1)
            load_x(0)
            for k in range(A_SLOTS, NB):
                load_a(0, k, True)
            with sp.Fori(0, NB - 1) as j:
                for k in range(NB):
                    load_a(j + 1, k, False, j)

            for s in range(NB):
                sp.wait_ge(b_out[s], 16 * NB)
            for m, i, j in use:
                s, nth, wait = plan[m, i, j]
                if not nth:
                    continue
                if wait and wait[0] == "gathered":
                    sp.wait_ge(t_ready, Q * NB * NB)
                    sp.wait_ge(a_summed, NB * NB)
                else:
                    sp.wait_ge({"av_step": av_step, "blk_used": blk_used, "defer_done": defer_done}[wait[0]], wait[1])
                sp.dma_start(flat(s), turned[j, i]).then_inc(blk_in[s], 16)
            for i in end_order(5):
                store_out(sp, i)
            sp.wait_ge(out_done, 16 * NB)

        @block_ctx.gpsimd
        def _(pool_eng):
            steps = [0]

            def step(ins):
                steps[0] += 1
                ins.then_inc(consts_step, 1)
                pool_eng.wait_ge(consts_step, steps[0])

            nc.gpsimd.memset(part[:, 0, :], 0.0).then_inc(zeros, 1)
            step(nc.gpsimd.memset(ident[:, :], 0.0))
            step(nc.gpsimd.affine_select(out=ident[:, :], in_=ident[:, :], compare_op=ALU.not_equal, fill=1.0,
                                         base=0, pattern=[[-1, P]], channel_multiplier=1))
            nc.gpsimd.tensor_tensor(fold[:, :], ident[:, 0:D], ident[:, D:P], ALU.add).then_inc(consts, 1)
            pool_eng.wait_ge(consts, 1)
            step(nc.gpsimd.memset(minus_half[:, :], -0.5))

            for s in range(NC):
                c = slice(CH * (NC - 1 - s), CH * (NC - s))
                m2, h0 = rdeg[:, c], S[:, c, EVEN, :]
                pool_eng.wait_ge(h0_asked, s + 1)
                step(nc.gpsimd.tensor_tensor(m2, m2, minus_half[:, :], ALU.pow))
                nc.gpsimd.tensor_tensor(h0, h0, m2.unsqueeze(2).to_broadcast([P, CH, D]), ALU.mult).then_inc(h0_ready, 1)

            pool_eng.wait_ge(small_in, 16 * 9)
            step(nc.gpsimd.tensor_tensor(r_end[lane(0), D:], wc[lane(0), 2, :], wc[lane(0), 2, :], ALU.add))
            step(nc.gpsimd.tensor_tensor(r_end[lane(1), D:], wc[lane(1), 1, :], wc[lane(1), 3, :], ALU.subtract))
            step(nc.gpsimd.tensor_tensor(r_w3[lane(1), :], wc[lane(1), 3, :], wc[lane(1), 3, :], ALU.add))
            step(nc.gpsimd.tensor_tensor(r_aux[:, :], wc[lane(0), 0, :], wc[lane(0), 2, :], ALU.subtract))
            nc.gpsimd.tensor_copy(r_end[:, 0:D], fold[:, :]).then_inc(consts, 1)

            pool_eng.wait_ge(h0_ready, NC)
            step(nc.gpsimd.tensor_tensor(X[:, :, :], X[:, :, :], S[:, :, EVEN, :], ALU.add))
            nc.gpsimd.tensor_tensor(X[:, :, :], X[:, :, :], beta[:, :].unsqueeze(1).to_broadcast([P, NT, D]),
                                    ALU.add).then_inc(residual, 1)

            tiles = [u.stop - u.start for u in H_UNITS for _ in range(3)] + [Q] * (2 * NB)
            for k, width in enumerate(tiles):
                m2 = st2[:, 0:width]
                pool_eng.wait_ge(root_asked, k + 1)
                nc.gpsimd.tensor_tensor(m2, m2, minus_half[:, 0:m2.shape[1]], ALU.pow).then_inc(root_done, 1)

        @block_ctx.tensor
        def _(pe):
            mm = nc.tensor.matmul

            def turn_h0(s):
                m = NC - 1 - s
                pe.wait_ge(h0_ready, s + 1)
                for k in range(CH):
                    ins = nc.tensor.transpose(ps[0:D, k // Q, (k % Q) * P:(k % Q + 1) * P],
                                              S[:, CH * m + k, EVEN, :], ident[:, :])
                ins.then_inc(h0_turned, 1)

            def mul_h0(s):
                m = NC - 1 - s
                pe.wait_ge(h0_copied, s + 1)
                if s:
                    pe.wait_ge(e_ready, s)
                for k in range(CH):
                    ins = mm(ps[:, 2, D * k:D * k + D], hT[:, k // Q, (k % Q) * P:(k % Q + 1) * P],
                             w_ui[:, int(m >= NU // (CH * P)), :], start=True, stop=True)
                ins.then_inc(h0_w, 1)

            def add_v(J, k, first):
                pe.wait_ge(a_in[k % A_SLOTS], 16 * (2 * J + k // A_SLOTS + 1))
                for q in range(Q):
                    ins = mm(ps[lane(q % 2), V_BANK, :], S[:, Q * ORDER[k] + q, ODD, :], pool[:, NB + k % A_SLOTS, q, :],
                             start=(k == 0 and q < 2), stop=(k == NB - 1 and q >= 2), skip_group_check=True)
                if k == NB - 1:
                    ins.then_inc(v_done, 1)
                elif first and k < NB - A_SLOTS:
                    ins.then_inc(v_added, 1)

            def turn_tiles(J, k, g, first):
                for qj in (2 * g, 2 * g + 1):
                    c = Q * k + qj
                    if c >= 2 or not first:
                        pe.wait_ge((even_copied, odd_copied)[c % 2], 2 * NB * J + c // 2)
                    for qi in range(Q):
                        ins = nc.tensor.transpose(ps[:, T_BANKS[c % 2], qi * P:(qi + 1) * P],
                                                  pool[:, NB + k % A_SLOTS, qi, qj * P:(qj + 1) * P], ident[:, :])
                    ins.then_inc(t_ready, 1)

            def turn_v(J):
                pe.wait_ge(even_copied, 2 * NB * J + 2 * NB - 1)
                pe.wait_ge(vt_copied, J + 1)
                for q in range(Q):
                    ins = mm(ps[:, T_BANKS[0], D * q:D * q + D], vT[:, 0, q * P:(q + 1) * P], fold[:, :],
                             start=True, stop=True)
                ins.then_inc(v_turned, 1)
                pe.wait_ge(v_ready, J + 1)

            def add_av(m, q0, q1):
                for q in range(q0, q1):
                    for n in (2 * m, 2 * m + 1):
                        ins = mm(ps[lane(n % 2), m, :], v_rows[:, q, :], pool[:, n, q, :],
                                 start=False, stop=False, skip_group_check=True)
                if q1 == Q:
                    ins.then_inc(av_step, 1)

            def panel(J, first):
                for s in range(NC):
                    m = NC - 1 - s
                    k = 2 * s
                    if first and s == 0:
                        pe.wait_ge(a_in[0], 16)
                        turn_tiles(J, 0, 0, first)
                        turn_h0(0)
                        pe.wait_ge(gather_in, 16 * 6)
                        nc.tensor.transpose(ps[:, 3, 0:NT], diag_rows[:, :], ident[0:NT, 0:NT]).then_inc(diag_turned, 1)
                        turn_tiles(J, 0, 1, first)
                        mul_h0(0)
                        pe.wait_ge(a_in[1], 16)
                        turn_tiles(J, 1, 0, first)
                        pe.wait_ge(e_ready, 1)
                        add_v(J, 0, first)
                        turn_h0(1)
                        add_v(J, 1, first)
                        mul_h0(1)
                        turn_tiles(J, 1, 1, first)
                        continue
                    if first:
                        pe.wait_ge(e_ready, s + 1)
                    add_v(J, k, first)
                    if first and s < NC - 1:
                        turn_h0(s + 1)
                    turn_tiles(J, k, 0, first)
                    if first and s < NC - 1:
                        mul_h0(s + 1)
                    add_v(J, k + 1, first)
                    turn_tiles(J, k, 1, first)
                    if s < NC - 1:
                        if not first:
                            add_av(m - 1, 0, Q // 2)
                        turn_tiles(J, k + 1, 0, first)
                        if not first:
                            add_av(m - 1, Q // 2, Q)
                        turn_tiles(J, k + 1, 1, first)
                    else:
                        turn_tiles(J, k + 1, 0, first)
                        if first:
                            pe.wait_ge(zeros, 1)
                            for c in range(NC):
                                for h in range(2):
                                    mm(ps[lane(h), c, :], part[:, 0, 0:D], part[:, 0, :], start=True, stop=False,
                                       skip_group_check=True)
                        turn_v(J)
                        turn_tiles(J, k + 1, 1, first)
                        add_av(NC - 1, 0, Q)

            pe.wait_ge(consts, 1)
            panel(0, True)
            with pe.Fori(1, NB) as J:
                panel(J, False)
            pe.wait_ge(even_copied, 2 * NB * NB)
            pe.wait_ge(odd_copied, 2 * NB * NB)

            def turn_av(k):
                pe.wait_ge(gt_copied, k + 1)
                if k >= 2:
                    pe.wait_ge(g_ready, k - 1)
                for q in range(Q):
                    ins = nc.tensor.transpose(ps[:, T_BANKS[k % 2], q * P:(q + 1) * P],
                                              yT[:, k % 2, q * P:(q + 1) * P], ident[:, :])
                ins.then_inc(g_turned, 1)

            for k in range(NC):
                if k:
                    add_av(NC - 1 - k, 0, Q)
                    turn_av(k - 1)
            turn_av(NC - 1)

            def wait_block(m, i, j):
                s, nth, _ = plan[m, i, j]
                if nth:
                    pe.wait_ge(blk_in[s], 16 * nth)
                return pool[:, s, :, :]

            def bank_of(m, i):
                return ACC_BANKS[PANELS.index((m, i)) % len(ACC_BANKS)]

            def wait_bank(m, i):
                k = PANELS.index((m, i))
                if k == 0:
                    pe.wait_ge(vt_copied, NB)
                elif k < len(ACC_BANKS):
                    pe.wait_ge(gt_copied, k)
                else:
                    m0, r = PANELS[k - len(ACC_BANKS)]
                    if m0:
                        pe.wait_ge(y_ready, ended(m0 + 1, r))
                    if m0 == 4:
                        pe.wait_ge(y_upper, half_rows(4).index(r) + 1)
                    elif m0 % 2 and r == NB - 1:
                        pe.wait_ge(y_ready, ended(m0 + 2, r))
                    else:
                        pe.wait_ge(part_saved, saved(m0, r))

            def operands(t):
                return S[:, t, ODD:EVEN + 1, :].rearrange("p k d -> p (k d)")

            def off_diagonal(m, i, j, used=True):
                cols = half_cols(m, i)
                start, stop = j == cols[0], j == cols[-1] and m % 2 == 0
                b = wait_block(m, i, j)
                if start:
                    wait_bank(m, i)
                if m == 0:
                    pe.wait_ge(h_ready, h_there(j))
                else:
                    pe.wait_ge(op_ready, ended(min(m, 3) + 1, j))
                for q in range(Q):
                    if m == 4:
                        ins = mm(ps[lane(q % 2), bank_of(m, i), :], S[:, Q * j + q, ODD, :], b[:, q, :],
                                 start=start and q < 2, stop=stop and q >= 2, skip_group_check=True)
                    else:
                        ins = mm(ps[:, bank_of(m, i), :], operands(Q * j + q), b[:, q, :],
                                 start=start and q == 0, stop=stop and q == Q - 1, skip_group_check=True)
                if used:
                    ins.then_inc(blk_used, 1)

            def add_p1(i, j):
                b = wait_block(p1_half(i), i, j)
                p = P1_ORDER.index(i)
                if j == 0:
                    pe.wait_ge(y1_ready, p) if p else pe.wait_ge(gt_copied, 3)
                    if p:
                        pe.wait_ge(y1_upper, p)
                pe.wait_ge(h1_kept, h_there(j))
                for q in range(Q):
                    ins = mm(ps[lane(q % 2), P1_BANK, :], S[:, Q * j + q, H1, :], b[:, q, :],
                             start=j == 0 and q < 2, stop=j == i and q >= 2, skip_group_check=True)
                if j == i:
                    ins.then_inc(p1_done, 1)
                return ins

            def on_diagonal(m, i):
                if i < NB:
                    b = wait_block(m, i, i)
                    pe.wait_ge(op_ready, ended(m, i)) if m > 1 else pe.wait_ge(h_ready, h_there(i))
                    if i == 0:
                        wait_bank(m, i)
                if i > 0:
                    d = wait_block(m, i - 1, i - 1)
                    pe.wait_ge(op_ready, ended(m + 1, i - 1))
                for q in range(Q):
                    if i < NB:
                        ins = mm(ps[lane(1), bank_of(m, i), :], S[:, Q * i + q, EVEN, :], b[:, q, :],
                                 start=(i == 0 and q == 0), stop=(q == Q - 1), skip_group_check=True)
                        if q == Q - 1:
                            ins.then_inc(acc_done, 1)
                    if i > 0:
                        ins = mm(ps[lane(0), bank_of(m, i - 1), :], S[:, Q * (i - 1) + q, ODD, :], d[:, q, :],
                                 start=(i == 1 and q == 0), stop=(q == Q - 1), skip_group_check=True)
                        if q == Q - 1:
                            ins.then_inc(defer_done, 1)

            def end_rows(n, i):
                c = ended(n, i)
                pe.wait_ge(y_ready, c)
                if n == 5 and i < NB - 1:
                    pe.wait_ge(y_upper, half_rows(4).index(i) + 1)
                if c > 2:
                    pe.wait_ge(rows_read, c - 2)
                sl, rhs = {
                    2: (lane(1), r_end[:, :]),
                    3: (lane(0), r_end[:, :]),
                    4: (lane(1), r_w3[:, :]),
                    5: (slice(0, P) if i < NB - 1 else lane(0), r_sage[:, :]),
                }[n]
                w = rhs.shape[1]
                for q in range(Q):
                    ins = mm(ps[:, T_BANKS[c % 2], P * q:P * q + w], yT[sl, c % 2, q * P:(q + 1) * P], rhs[sl, :],
                             start=True, stop=True)
                ins.then_inc(rows_ready, 1)

            def aux_turn(u):
                i = u if u < NB else end_order(5)[u - NB]
                if u:
                    pe.wait_ge(ht_copied, u)
                else:
                    pe.wait_ge(gt_copied, 4)
                pe.wait_ge(h_ready, h_there(i)) if u < NB else pe.wait_ge(op_ready, ended(4, i))
                for q in range(Q):
                    ins = nc.tensor.transpose(ps[0:D, HT_BANK, q * P:(q + 1) * P],
                                              S[:, Q * i + q, EVEN if u < NB else ODD, :], ident[:, :])
                ins.then_inc(ht_done, 1)

            def p1_rows(i):
                p = P1_ORDER.index(i)
                pe.wait_ge(y1_ready, p + 1)
                pe.wait_ge(y1_upper, p + 1)
                return y1[:, p % 2, :]

            def aux_mul(u):
                number = aux_number("h2", u) if u < NB else aux_number("h3", u - NB)
                pe.wait_ge(ht_copied, u + 1)
                pe.wait_ge(aux_read, number) if u else pe.wait_ge(gt_copied, NC)
                y = p1_rows(u) if u < NB and u not in P1_LATE else None
                for q in range(Q):
                    tile = slice(q * P, (q + 1) * P)
                    h, rows_q = hT[:, u % 2, tile], ps[:, AUX_BANK, tile]
                    if u < NB:
                        ins = mm(rows_q[:, 0:D], h, r_aux[:, :], start=True, stop=True)
                    else:
                        ins = mm(rows_q, h, r_sage_aux[:, :, :].rearrange("p k d -> p (k d)"), start=True, stop=True)
                    if y is not None:
                        ins = mm(rows_q[:, D:], y[:, tile], fold[:, :], start=True, stop=True)
                ins.then_inc(aux_done, 1)

            def aux_p1(i):
                pe.wait_ge(aux_read, aux_number("P1", i))
                y = p1_rows(i)
                for q in range(Q):
                    ins = mm(ps[:, AUX_BANK, q * P + D:(q + 1) * P], y[:, q * P:(q + 1) * P], fold[:, :],
                             start=True, stop=True)
                ins.then_inc(aux_done, 1)

            pe.wait_ge(consts, 2)
            for i, j in first_blocks():
                off_diagonal(0, i, j)

            def end_p2(i):
                end_rows(2, i)
                aux_turn(i)
                if i:
                    aux_mul(i - 1)

            for i in half_rows(1):
                if i == 1:
                    end_p2(0)
                elif i:
                    off_diagonal(1, i, 0, used=i in P1_LATE)
                    end_p2(i - 1)
                for j in range(i):
                    if i in P1_LATE:
                        if j:
                            off_diagonal(1, i, j)
                    elif j == i - 1:
                        add_p1(i, j)
                        add_p1(i, i)
                        off_diagonal(1, i, j)
                    elif j:
                        add_p1(i, j)
                        off_diagonal(1, i, j)
                    else:
                        add_p1(i, 0).then_inc(blk_used, 1)
                on_diagonal(1, i)
                if i == 0:
                    add_p1(0, 0)
            end_p2(NB - 1)
            on_diagonal(1, NB)
            aux_mul(NB - 1)

            end_rows(3, NB - 1)
            for i in half_rows(2):
                for idx, j in enumerate(half_cols(2, i)):
                    off_diagonal(2, i, j)
                    if idx == 0 and i < NB - 2:
                        end_rows(3, i + 1)
            end_rows(3, 0)

            for i in half_rows(3):
                for k, b in enumerate(late_p1(i) if i < 2 else []):
                    add_p1(*b)
                    if i == 1 and k == 0:
                        end_rows(4, 0)
                if i == 2:
                    add_p1(*late_p1(2)[0])
                    end_rows(4, 1)
                for j in half_cols(3, i):
                    off_diagonal(3, i, j)
                    if i == 2 and j == 0:
                        add_p1(*late_p1(2)[1])
                    if j == 0 and i > 2:
                        end_rows(4, i - 1)
                        if i in (3, 5):
                            aux_p1(P1_LATE[(i - 3) // 2])
                on_diagonal(3, i)

            for k, i in enumerate(half_rows(4)):
                for idx, j in enumerate(half_cols(4, i)):
                    off_diagonal(4, i, j)
                    if idx == 0 and k == 0:
                        end_rows(4, NB - 1)
                        aux_turn(NB)
                    elif idx == 0:
                        if k == 1:
                            end_rows(5, 0)
                            aux_turn(NB + 1)
                        aux_mul(NB + k)
                        end_rows(5, end_order(5)[k])
                        aux_turn(NB + k + 1)
                if k == 0:
                    on_diagonal(3, NB)
                    aux_mul(NB)
            aux_mul(2 * NB - 1)
            end_rows(5, end_order(5)[-1])

        @block_ctx.scalar
        def _(act):
            def copy_h0(s):
                act.wait_ge(h0_turned, s + 1)
                if s:
                    act.wait_ge(h0_w, s)
                nc.scalar.copy(hT[:, :, :], ps[0:D, 0:2, :]).then_inc(h0_copied, 1)

            def panel(J, first):
                for k in range(NB):
                    s, n = k // 2, ORDER[k]
                    if not first:
                        act.wait_ge(av_step, NC * J - (NC - 1 - s))
                        act.wait_ge(b_out[n], 16 * J)
                    for qj in range(Q):
                        c = Q * k + qj
                        if first and c in (2, Q + 2):
                            copy_h0(k)
                        elif first and c >= CH and c % CH == 0 and s < NC - 1:
                            copy_h0(s + 1)
                        if qj % 2 or first:
                            act.wait_ge(t_ready, Q * NB * J + c + 1)
                            nc.scalar.copy(pool[:, n, qj, :], ps[:, T_BANKS[qj % 2], :]).then_inc(
                                (even_copied, odd_copied)[qj % 2], 1)
                        if c == Q * NB - 7:
                            act.wait_ge(v_done, J + 1)
                            nc.scalar.copy(vT[:, 0, :], ps[:, V_BANK, :]).then_inc(vt_copied, 1)
                    act.wait_ge(even_copied, 2 * NB * J + 2 * k + 2)
                    act.wait_ge(odd_copied, 2 * NB * J + 2 * k + 2)
                    act.dma_start(turned_panel(J, n), flat(n)).then_inc(b_out[n], 16)

            panel(0, True)
            with act.Fori(1, NB) as J:
                panel(J, False)

            def copy_gt(k):
                act.wait_ge(av_step, NC * (NB - 1) + k + 1)
                if k >= 2:
                    act.wait_ge(g_turned, k - 1)
                nc.scalar.copy(yT[:, k % 2, :], ps[:, NC - 1 - k, :]).then_inc(gt_copied, 1)

            def copy_g(k):
                act.wait_ge(g_turned, k + 1)
                act.wait_ge(v_done, NB)
                c = slice(CH * (NC - 1 - k), CH * (NC - k))
                nc.scalar.copy(S[:, c, ODD, :].rearrange("p (b q) d -> p b q d", b=2),
                               ps[:, T_BANKS[k % 2], :].rearrange("p (q b d) -> p b q d", q=Q, b=2)).then_inc(g_ready, 1)

            for k in range(NC):
                copy_gt(k)
                if k:
                    copy_g(k - 1)
            copy_g(NC - 1)

            def acc_bank(m, i):
                return ACC_BANKS[PANELS.index((m, i)) % len(ACC_BANKS)]

            def save(m, i):
                if m % 2:
                    act.wait_ge(defer_done, l_count(m, i))
                    if m == 1 and i in P1_LATE:
                        act.wait_ge(part_saved, saved(0, i))
                        k = P1_LATE.index(i)
                        nc.scalar.copy(p1_kept[:, k, :], part[lane(0), i, :]).then_inc(late_kept, 1)
                        act.wait_ge(late_kept, k + 1)
                    elif m == 1:
                        act.wait_ge(y1_ready, P1_ORDER.index(i) + 1)
                    h = lane(0)
                else:
                    act.wait_ge(blk_used, used_no[m, i, i + 1])
                    h = lane(1) if m else slice(0, P)
                nc.scalar.copy(part[h, i, :], ps[h, acc_bank(m, i), :]).then_inc(part_saved, 1)

            def upper_p1(i):
                p = P1_ORDER.index(i)
                act.wait_ge(p1_done, p + 1)
                if p >= 2:
                    act.wait_ge(aux_done, p1_aux(P1_ORDER[p - 2]) + 1)
                nc.scalar.copy(y1[lane(1), p % 2, :], ps[lane(1), P1_BANK, :]).then_inc(y1_upper, 1)

            def upper_p5(i):
                c = ended(5, i)
                act.wait_ge(rows_ready, c - 2)
                act.wait_ge(blk_used, used_no[4, i, half_cols(4, i)[-1]])
                nc.scalar.copy(yT[lane(1), c % 2, :], ps[lane(1), acc_bank(4, i), :]).then_inc(y_upper, 1)

            def copy_ht(u):
                act.wait_ge(ht_done, u + 1)
                if u >= 2:
                    act.wait_ge(aux_done, (u - 2 if u - 2 < NB else aux_number("h3", u - 2 - NB)) + 1)
                nc.scalar.copy(hT[:, u % 2, :], ps[0:D, HT_BANK, :]).then_inc(ht_copied, 1)

            def keep_h1(k):
                act.wait_ge(h_ready, k + 1)
                c = H_UNITS[k]
                nc.scalar.copy(S[:, c, H1, :], S[:, c, ODD, :]).then_inc(h1_kept, 1)

            for i in half_rows(0):
                save(0, i)
                if i < len(H_UNITS):
                    keep_h1(len(H_UNITS) - 1 - i)
            for i in half_rows(1):
                if i:
                    copy_ht(i - 1)
                if i not in P1_LATE:
                    upper_p1(i)
                if i:
                    save(1, i - 1)
            copy_ht(NB - 1)
            for i in half_rows(2):
                save(2, i)
            for i in range(NB - 1):
                if i < len(P1_LATE):
                    upper_p1(P1_LATE[i])
                save(3, i)
            act.wait_ge(y1_ready, NB)
            for k, i in enumerate(end_order(5)):
                copy_ht(NB + k)
                if i < NB - 1:
                    upper_p5(i)
                act.wait_ge(aux_done, aux_number("h3", k) + 1)
                if k >= 2:
                    act.wait_ge(fin_step, k - 1)
                nc.scalar.copy(g[:, k % 2, :, :].rearrange("p t d -> p (t d)"), ps[:, AUX_BANK, :]).then_inc(aux_read, 1)

        @block_ctx.vector
        def _(dve):
            vec = nc.vector
            steps = [0]

            def step(ins):
                steps[0] += 1
                ins.then_inc(dve_step, 1)
                dve.wait_ge(dve_step, steps[0])

            roots = [0]

            def wait_root():
                roots[0] += 1
                dve.wait_ge(root_done, roots[0])

            def cols(stat, t):
                return stat.unsqueeze(2).to_broadcast([P, t, D])

            def rows(vecs, t):
                return vecs.unsqueeze(1).to_broadcast([P, t, D])

            def centre(src, a, m2, t):
                b, m1 = tmp2[:, 0:t, :], st1[:, 0:t]
                step(vec.tensor_reduce(m1, src, AX.X, ALU.add))
                step(vec.scalar_tensor_tensor(out=a, in0=cols(m1, t), scalar=-1.0 / D, in1=src, op0=ALU.mult, op1=ALU.add))
                step(vec.tensor_tensor(b, a, a, ALU.mult))
                step(vec.tensor_reduce(m2, b, AX.X, ALU.add))
                return vec.tensor_scalar(m2, m2, D * EPS, None, ALU.add)

            def relu8(a):
                return vec.tensor_scalar(a, a, 8.0, 0.0, ALU.mult, ALU.max)

            def normalise(src, dst, scale, t):
                a, m2 = tmp[:, 0:t, :], st2[:, 0:t]
                centre(src, a, m2, t).then_inc(root_asked, 1)
                step(scale(a))
                wait_root()
                return vec.tensor_tensor(dst, a, cols(m2, t), ALU.mult)

            def relu_norm(src, dst, t):
                return normalise(src, dst, relu8, t)

            def make_h0(s):
                m = NC - 1 - s
                c = slice(CH * m, CH * m + CH)
                dve.wait_ge(x_in[m], 16)
                h0 = S[:, c, EVEN, :]
                step(centre(X[:, c, :], h0, rdeg[:, c], CH))
                relu8(h0).then_inc(h0_asked, 1)

            def make_e(s):
                m = NC - 1 - s
                c = slice(CH * m, CH * m + CH)
                dve.wait_ge(h0_w, s + 1)
                dve.wait_ge(h0_ready, s + 1)
                step(vec.tensor_tensor(tmp[:, :, :], ps[:, 2, :].rearrange("p (t d) -> p t d", t=CH),
                                       cols(cdiag[:, c], CH), ALU.mult))
                vec.tensor_tensor(S[:, c, ODD, :], tmp[:, :, :], S[:, c, EVEN, :], ALU.add).then_inc(e_ready, 1)
                dve.wait_ge(e_ready, s + 1)

            def scale_diag():
                dve.wait_ge(gather_in, 16 * 6)
                step(vec.tensor_tensor(cpar[:, :], pars[:, 0:4:2], pars[:, 1:4:2], ALU.mult))
                dve.wait_ge(diag_turned, 1)
                nu = NU // P
                step(vec.tensor_scalar(cdiag[:, 0:nu], ps[:, 3, 0:nu], cpar[:, 0:1], None, ALU.mult))
                step(vec.tensor_scalar(cdiag[:, nu:], ps[:, 3, nu:NT], cpar[:, 1:2], None, ALU.mult))

            def sum_rows(J, k, q):
                if q == 0:
                    dve.wait_ge(a_in[k % A_SLOTS], 16 * (2 * J + k // A_SLOTS + 1))
                return vec.tensor_reduce(rs_part[:, ORDER[k], q:q + 2], pool[:, NB + k % A_SLOTS, q:q + 2, :], AX.X,
                                         ALU.add)

            def add_sums(J, k, ins):
                ins.then_inc(a_summed, 1)
                dve.wait_ge(a_summed, NB * J + k + 1)
                r = rowsum[:, Q * ORDER[k]:Q * ORDER[k] + Q]
                vec.tensor_tensor(r, r, rs_part[:, ORDER[k], :], ALU.add).then_inc(rs_added, 1)

            def sum_first(k):
                sum_rows(0, k, 0)
                add_sums(0, k, sum_rows(0, k, 2))

            def copy_v(J):
                dve.wait_ge(v_turned, J + 1)
                vec.tensor_copy(part[:, 1, 0:Q * D], ps[:, T_BANKS[0], 0:Q * D]).then_inc(v_ready, 1)

            step(vec.memset(rowsum[:, :], 0.0))
            make_h0(0)
            sum_first(0)
            make_h0(1)
            scale_diag()
            for s in range(NC):
                make_e(s)
                if s:
                    sum_first(2 * s)
                if s < NC - 2:
                    make_h0(s + 2)
                sum_first(2 * s + 1)
            copy_v(0)
            with dve.Fori(1, NB) as J:
                for k in range(NB):
                    s, n = k // 2, ORDER[k]
                    dve.wait_ge(av_step, NC * J - (NC - 1 - s))
                    dve.wait_ge(b_out[n], 16 * J)
                    for h in range(2):
                        c = Q * k + 2 * h
                        if c == Q * NB - 2:
                            copy_v(J)
                        dve.wait_ge(t_ready, Q * NB * J + c + 1)
                        vec.tensor_copy(pool[:, n, 2 * h, :], ps[:, T_BANKS[0], :]).then_inc(even_copied, 1)
                        if h == 0:
                            dve.wait_ge(rs_added, NB * J - (NB - 1 - k))
                        ins = sum_rows(J, k, 2 * h)
                    add_sums(J, k, ins)

            dve.wait_ge(rs_added, NB * NB)
            step(vec.tensor_scalar(rdeg[:, :], rowsum[:, :], 1.0, 1.0, ALU.add, ALU.max))
            step(vec.reciprocal(rdeg[:, :], rdeg[:, :]))

            dve.wait_ge(small_in, 16 * 9)
            step(vec.tensor_scalar(gamma8[:, :], gamma8[:, :], 8.0, None, ALU.mult))
            dve.wait_ge(residual, 1)
            for k, c in enumerate(H_UNITS):
                t = c.stop - c.start
                x_c, h1, a = X[:, c, :], S[:, c, ODD, :], tmp[:, 0:t, :]
                dve.wait_ge(g_ready, NC - c.start // CH)
                step(normalise(h1, a, lambda a: vec.tensor_tensor(a, a, rows(gamma8[:, :], t), ALU.mult), t))
                step(vec.tensor_tensor(x_c, x_c, a, ALU.add))
                step(relu_norm(x_c, h1, t))
                step(vec.scalar_tensor_tensor(out=x_c, in0=h1, scalar=-0.1, in1=x_c, op0=ALU.mult, op1=ALU.add))
                relu_norm(x_c, S[:, c, EVEN, :], t).then_inc(h_ready, 1)
                dve.wait_ge(h_ready, k + 1)

            def end_p1(i):
                p = P1_ORDER.index(i)
                dve.wait_ge(p1_done, p + 1)
                if p >= 2:
                    dve.wait_ge(aux_done, p1_aux(P1_ORDER[p - 2]) + 1)
                acc, y = ps[lane(0), P1_BANK, :], y1[lane(0), p % 2, :]
                if i in P1_LATE:
                    dve.wait_ge(late_kept, P1_LATE.index(i) + 1)
                    vec.tensor_tensor(y, acc, p1_kept[:, P1_LATE.index(i), :], ALU.add).then_inc(y1_ready, 1)
                elif i < NB - 1:
                    dve.wait_ge(part_saved, saved(0, i))
                    vec.tensor_tensor(y, acc, part[lane(0), i, :], ALU.add).then_inc(y1_ready, 1)
                else:
                    vec.tensor_copy(y, acc).then_inc(y1_ready, 1)

            def end_sum(n, i):
                c = ended(n, i)
                h = lane(n % 2 == 0)
                m = n - 1
                if n % 2 and i == NB - 1:
                    m -= 1
                    dve.wait_ge(defer_done, l_count(m, i))
                elif n % 2:
                    dve.wait_ge(blk_used, used_no[m, i, half_cols(m, i)[-1]])
                else:
                    dve.wait_ge(acc_done, l_count(m, i))
                if c > 2:
                    dve.wait_ge(rows_ready, c - 2)
                acc = ps[h, ACC_BANKS[PANELS.index((m, i)) % len(ACC_BANKS)], :]
                if i < NB - 1:
                    dve.wait_ge(part_saved, saved(m - 1, i))
                    vec.tensor_tensor(yT[h, c % 2, :], acc, part[h, i, :], ALU.add).then_inc(y_ready, 1)
                else:
                    vec.tensor_copy(yT[h, c % 2, :], acc).then_inc(y_ready, 1)

            def end_layer(n, i):
                c = ended(n, i)
                ti = slice(Q * i, Q * i + Q)
                x_i, odd, even = X[:, ti, :], S[:, ti, ODD, :], S[:, ti, EVEN, :]
                r = ps[:, T_BANKS[c % 2], :].rearrange("p (q k d) -> p q k d", q=Q, k=2)
                r0, r1 = r[:, :, 0, :], r[:, :, 1, :]
                a, b, m1 = tmp[:, 0:Q, :], tmp2[:, 0:Q, :], st1[:, 0:Q]
                if n == 5:
                    k = end_order(5).index(i)
                    dve.wait_ge(aux_read, aux_number("h3", k) + 1)
                    gi = g[:, k % 2, :, :].rearrange("p (q k) d -> p q k d", k=2)
                    step(vec.tensor_tensor(gi[:, :, 0, :], gi[:, :, 0, :], rows(b_sage[:, :], Q), ALU.add))
                dve.wait_ge(rows_ready, c)

                def read(ins):
                    ins.then_inc(rows_read, 1)
                    dve.wait_ge(rows_read, c)

                if n == 2:
                    vec.tensor_copy(odd, r0).then_inc(op_ready, 1)
                    read(vec.tensor_tensor(x_i, x_i, r1, ALU.add))
                elif n == 3:
                    vec.scalar_tensor_tensor(out=even, in0=r0, scalar=2.0, in1=even, op0=ALU.mult,
                                             op1=ALU.subtract).then_inc(op_ready, 1)
                    read(vec.tensor_tensor(x_i, x_i, r1, ALU.add))
                elif n == 4:
                    read(vec.tensor_tensor(x_i, x_i, r0, ALU.add))
                    relu_norm(x_i, odd, Q).then_inc(op_ready, 1)
                else:
                    read(vec.tensor_tensor(a, r0, gi[:, :, 1, :], ALU.add))
                    step(vec.tensor_tensor(a, a, cols(rdeg[:, ti], Q), ALU.mult))
                    step(vec.tensor_tensor(a, a, gi[:, :, 0, :], ALU.add))
                    step(vec.scalar_tensor_tensor(out=b, in0=a, scalar=0.0, in1=a, op0=ALU.max, op1=ALU.mult))
                    step(vec.tensor_reduce(m1, b, AX.X, ALU.add))
                    vec.tensor_scalar(st2[:, 0:Q], m1, 1e-24, None, ALU.max).then_inc(root_asked, 1)
                    wait_root()
                    step(vec.scalar_tensor_tensor(out=a, in0=a, scalar=0.0, in1=cols(st2[:, 0:Q], Q), op0=ALU.max,
                                                  op1=ALU.mult))
                    vec.tensor_tensor(x_i, x_i, a, ALU.add).then_inc(fin_step, 1)
                    dve.wait_ge(fin_step, k + 1)
                if n < 5:
                    dve.wait_ge(op_ready, c)

            def add_aux(i):
                ti = slice(Q * i, Q * i + Q)
                x_i = X[:, ti, :]
                aux = ps[:, AUX_BANK, :].rearrange("p (q k d) -> p q k d", q=Q, k=2)
                dve.wait_ge(aux_done, i + 1)
                ins = vec.tensor_tensor(x_i, x_i, aux[:, :, 0, :], ALU.add)
                if i in P1_LATE:
                    ins.then_inc(aux_read, 1)
                    dve.wait_ge(aux_read, i + 1)
                else:
                    step(ins)
                    add_ode(i, i)
                step(vec.tensor_tensor(x_i, x_i, rows(b_cheb[:, :], Q), ALU.add))

            def add_ode(i, number):
                ti = slice(Q * i, Q * i + Q)
                x_i, a, m1 = X[:, ti, :], tmp[:, 0:Q, :], st1[:, 0:Q]
                aux = ps[:, AUX_BANK, :].rearrange("p (q k d) -> p q k d", q=Q, k=2)
                dve.wait_ge(aux_done, number + 1)
                vec.tensor_tensor(a, aux[:, :, 1, :], S[:, ti, H1, :], ALU.mult).then_inc(aux_read, 1)
                dve.wait_ge(aux_read, number + 1)
                step(vec.tensor_reduce(m1, a, AX.X, ALU.add))
                step(vec.tensor_scalar(m1, m1, -0.01, 1.0, ALU.mult, ALU.add))
                step(vec.tensor_tensor(x_i, x_i, cols(m1, Q), ALU.add))

            dve.wait_ge(h1_kept, len(H_UNITS))
            for i in range(NB):
                if i == 0:
                    end_sum(2, i)
                if i not in P1_LATE:
                    end_p1(i)
                if i:
                    end_sum(2, i)
                end_layer(2, i)
                if i:
                    add_aux(i - 1)
            for i in end_order(3):
                end_sum(3, i)
                end_layer(3, i)
                if i == NB - 1:
                    add_aux(i)
            for i in end_order(4):
                end_sum(4, i)
                if i == 0:
                    end_p1(P1_LATE[0])
                end_layer(4, i)
                if i == 1:
                    end_p1(P1_LATE[1])
                if i in (2, 4):
                    late = P1_LATE[(i - 2) // 2]
                    add_ode(late, aux_number("P1", late))
            order = end_order(5)
            end_sum(5, order[0])
            for k, i in enumerate(order):
                if k < 5:
                    end_sum(5, order[k + 1])
                end_layer(5, i)
                if 5 <= k < NB - 1:
                    end_sum(5, order[k + 1])


_INS = ["x", "adj", "L0_gnn_W_u", "L0_gnn_diag_u", "L0_gnn_par_u", "L0_gnn_W_i", "L0_gnn_diag_i", "L0_gnn_par_i",
        "L0_gnn_ln_gamma", "L0_gnn_ln_beta", "L1_gnn_t", "L2_gnn_weight", "L2_gnn_bias", "L3_gnn_W", "L3_gnn_b"]


def kernel(**inputs):
    import numpy as _np
    import concourse.bacc as _bacc
    from concourse import mybir as _mybir
    from concourse.bass_utils import run_bass_kernel_spmd as _run

    nc = _bacc.Bacc("TRN2", target_bir_lowering=False, num_devices=1)
    arrays, args = {}, []
    for name in _INS:
        a = _np.ascontiguousarray(inputs[name])
        arrays[f"in_{name}"] = a
        args.append(nc.dram_tensor(f"in_{name}", a.shape, _mybir.dt.from_np(a.dtype), kind="ExternalInput").ap())
    args.append(nc.dram_tensor("out", (N, D), F32, kind="ExternalOutput").ap())
    graph_layers(nc, *args)
    r = _run(nc, [arrays], core_ids=[0])
    return r.results[0]["out"]
```
